# Optimizing a Trainium2 kernel written in Bass

```python
import numpy as np
import jax
import jax.numpy as jnp

def _softmax(x, axis=-1):
    return jax.nn.softmax(x, axis=axis)

def _gelu(x):
    return jax.nn.gelu(x, approximate=True)

def _silu(x):
    return jax.nn.silu(x)

def _sigmoid(x):
    return jax.nn.sigmoid(x)

def _layernorm(x, axis=-1, eps=1e-05):
    m = jnp.mean(x, axis=axis, keepdims=True)
    v = jnp.var(x, axis=axis, keepdims=True)
    return (x - m) / jnp.sqrt(v + eps)

def _scatter_add(tgt, idx, src, axis=0):
    return tgt.at[idx].add(src)

def _segment_sum(src, seg, n):
    return jax.ops.segment_sum(src, seg, n)
kernel_name = 'mk_recurrent_d1_jaxref_r8_862085'

def setup_inputs(seed: int=0):
    np.random.seed(seed)
    _w = jnp.asarray

    def _L0_attn_setup():
        import jax, jax.numpy as jnp
        import numpy as np
        NH, HS, K = (32, 256, 16)
        HD = HS // NH
        B, L = (4, 256)
        EPS = 1e-06

        def _ln(x, gamma, beta):
            mu = x.mean(-1, keepdims=True)
            var = x.var(-1, keepdims=True)
            return gamma * ((x - mu) / jnp.sqrt(var + EPS)) + beta

        def _ln_fused_l2_bwd(x, target, gamma, beta):
            D = x.shape[-1]
            mu = x.mean(-1, keepdims=True)
            std = jnp.sqrt(x.var(-1, keepdims=True) + EPS)
            xh = (x - mu) / std
            gxh = (gamma * xh + beta - target) * gamma
            return (D * gxh - gxh.sum(-1, keepdims=True) - xh * (gxh * xh).sum(-1, keepdims=True)) / (D * std)

        def _forward(hidden_states, q_w, k_w, v_w, o_w, W1, b1, ttt_norm_weight, ttt_norm_bias, ttt_lr_weight, ttt_lr_bias, learnable_token_idx, post_norm_weight, post_norm_bias):
            Bb, Ll, _ = hidden_states.shape
            NM = Ll // K

            def proj_heads(w):
                return (hidden_states @ w.T).reshape(Bb, Ll, NH, HD).transpose(0, 2, 1, 3)
            XQ = proj_heads(q_w).reshape(Bb, NH, NM, K, HD)
            XK = proj_heads(k_w).reshape(Bb, NH, NM, K, HD)
            XV = proj_heads(v_w).reshape(Bb, NH, NM, K, HD)
            X = hidden_states.reshape(Bb, NM, K, HS)
            ttt_lr = jnp.einsum('bnkc,hdc->bhnkd', X, ttt_lr_weight) + ttt_lr_bias.reshape(1, NH, 1, 1, 1)
            ttt_lr_eta = jax.nn.sigmoid(ttt_lr).transpose(0, 1, 2, 4, 3) / HD
            token_idx = jnp.clip(1.0 / jnp.arange(1, K + 1, dtype=jnp.float32) + learnable_token_idx, 0.0, None)
            eta = token_idx.reshape(1, 1, 1, K, 1) * ttt_lr_eta
            ln_w = ttt_norm_weight.reshape(NH, 1, HD)
            ln_b = ttt_norm_bias.reshape(NH, 1, HD)

            def step(carry, x):
                W1_s, b1_s = carry
                xq, xk, xv, eta_mb = x
                Z1 = xk @ W1_s + b1_s
                grad = _ln_fused_l2_bwd(Z1, xv - xk, ln_w, ln_b)
                Attn1 = jnp.tril(xq @ xk.swapaxes(-1, -2))
                b1_bar = b1_s - jnp.tril(eta_mb) @ grad
                Z1_bar = xq @ W1_s - eta_mb * Attn1 @ grad + b1_bar
                last_eta = eta_mb[:, :, -1, :, None]
                W1_new = W1_s - (last_eta * xk).swapaxes(-1, -2) @ grad
                b1_new = b1_s - jnp.sum(last_eta * grad, axis=-2, keepdims=True)
                out = xq + _ln(Z1_bar, ln_w, ln_b)
                return ((W1_new, b1_new), out)
            init = (jnp.tile(W1[None], (Bb, 1, 1, 1)), jnp.tile(b1[None], (Bb, 1, 1, 1)))
            xs = (XQ.transpose(2, 0, 1, 3, 4), XK.transpose(2, 0, 1, 3, 4), XV.transpose(2, 0, 1, 3, 4), eta.transpose(2, 0, 1, 3, 4))
            _, ys = jax.lax.scan(step, init, xs)
            out = ys.transpose(1, 0, 3, 2, 4).reshape(Bb, Ll, HS)
            out = _ln(out, post_norm_weight, post_norm_bias)
            return out @ o_w.T
        key = jax.random.key(seed)
        ks = jax.random.split(key, 8)
        s = 0.02
        return {'hidden_states': jax.random.normal(ks[0], (B, L, HS), jnp.float32), 'position_ids': jnp.tile(jnp.arange(L, dtype=jnp.int32)[None], (B, 1)), 'q_w': jax.random.normal(ks[1], (HS, HS), jnp.float32) * s, 'k_w': jax.random.normal(ks[2], (HS, HS), jnp.float32) * s, 'v_w': jax.random.normal(ks[3], (HS, HS), jnp.float32) * s, 'o_w': jax.random.normal(ks[4], (HS, HS), jnp.float32) * s, 'W1': jax.random.normal(ks[5], (NH, HD, HD), jnp.float32) * s, 'b1': jnp.zeros((NH, 1, HD), jnp.float32), 'ttt_norm_weight': jnp.ones((NH, HD), jnp.float32), 'ttt_norm_bias': jnp.zeros((NH, HD), jnp.float32), 'ttt_lr_weight': jax.random.normal(ks[6], (NH, 1, HS), jnp.float32) * s, 'ttt_lr_bias': jnp.zeros((NH, 1), jnp.float32), 'learnable_token_idx': jnp.zeros((K,), jnp.float32), 'post_norm_weight': jnp.ones((HS,), jnp.float32), 'post_norm_bias': jnp.zeros((HS,), jnp.float32)}
    _L0_attn_in = _L0_attn_setup()

    def _L0_ffn_setup():
        import jax, jax.numpy as jnp
        import numpy as np
        NUM_EXPERTS = 8
        TOP_K = 2
        MODEL_DIM = 256
        INTER_DIM = 128
        GATE_SCALE = 1.0
        UP_SCALE = 0.0
        key = jax.random.key(seed)
        k1, k2, k3, k4 = jax.random.split(key, 4)
        hidden_states = jax.random.normal(k1, (2, 256, MODEL_DIM), jnp.float32)
        router_gate = jax.random.normal(k2, (NUM_EXPERTS, MODEL_DIM), jnp.float32) * 0.02
        expert_gate_up = jax.random.normal(k3, (NUM_EXPERTS, MODEL_DIM, 2 * INTER_DIM), jnp.float32) * 0.02
        expert_down = jax.random.normal(k4, (NUM_EXPERTS, INTER_DIM, MODEL_DIM), jnp.float32) * 0.02
        return {'hidden_states': hidden_states, 'router_gate': router_gate, 'expert_gate_up': expert_gate_up, 'expert_down': expert_down}
    _L0_ffn_in = _L0_ffn_setup()
    _d = {'L0_attn_hidden_states': _L0_attn_in['hidden_states'], 'L0_attn_position_ids': _L0_attn_in['position_ids'], 'L0_attn_q_w': _L0_attn_in['q_w'], 'L0_attn_k_w': _L0_attn_in['k_w'], 'L0_attn_v_w': _L0_attn_in['v_w'], 'L0_attn_o_w': _L0_attn_in['o_w'], 'L0_attn_W1': _L0_attn_in['W1'], 'L0_attn_b1': _L0_attn_in['b1'], 'L0_attn_ttt_norm_weight': _L0_attn_in['ttt_norm_weight'], 'L0_attn_ttt_norm_bias': _L0_attn_in['ttt_norm_bias'], 'L0_attn_ttt_lr_weight': _L0_attn_in['ttt_lr_weight'], 'L0_attn_ttt_lr_bias': _L0_attn_in['ttt_lr_bias'], 'L0_attn_learnable_token_idx': _L0_attn_in['learnable_token_idx'], 'L0_attn_post_norm_weight': _L0_attn_in['post_norm_weight'], 'L0_attn_post_norm_bias': _L0_attn_in['post_norm_bias'], 'L0_ffn_router_gate': _L0_ffn_in['router_gate'], 'L0_ffn_expert_gate_up': _L0_ffn_in['expert_gate_up'], 'L0_ffn_expert_down': _L0_ffn_in['expert_down']}
    _x0 = _d['L0_attn_hidden_states']
    _d['L0_attn_hidden_states'] = jax.random.normal(jax.random.fold_in(jax.random.key(seed), 1), (4, 256, 256), dtype=_x0.dtype)
    del _x0
    return _d

def reference(L0_attn_hidden_states, L0_attn_position_ids, L0_attn_q_w, L0_attn_k_w, L0_attn_v_w, L0_attn_o_w, L0_attn_W1, L0_attn_b1, L0_attn_ttt_norm_weight, L0_attn_ttt_norm_bias, L0_attn_ttt_lr_weight, L0_attn_ttt_lr_bias, L0_attn_learnable_token_idx, L0_attn_post_norm_weight, L0_attn_post_norm_bias, L0_ffn_router_gate, L0_ffn_expert_gate_up, L0_ffn_expert_down):

    def _L0_attn_ref(hidden_states, position_ids, q_w, k_w, v_w, o_w, W1, b1, ttt_norm_weight, ttt_norm_bias, ttt_lr_weight, ttt_lr_bias, learnable_token_idx, post_norm_weight, post_norm_bias):
        import jax, jax.numpy as jnp
        import numpy as np
        NH, HS, K = (32, 256, 16)
        HD = HS // NH
        B, L = (4, 256)
        EPS = 1e-06

        def _ln(x, gamma, beta):
            mu = x.mean(-1, keepdims=True)
            var = x.var(-1, keepdims=True)
            return gamma * ((x - mu) / jnp.sqrt(var + EPS)) + beta

        def _ln_fused_l2_bwd(x, target, gamma, beta):
            D = x.shape[-1]
            mu = x.mean(-1, keepdims=True)
            std = jnp.sqrt(x.var(-1, keepdims=True) + EPS)
            xh = (x - mu) / std
            gxh = (gamma * xh + beta - target) * gamma
            return (D * gxh - gxh.sum(-1, keepdims=True) - xh * (gxh * xh).sum(-1, keepdims=True)) / (D * std)

        def _forward(hidden_states, q_w, k_w, v_w, o_w, W1, b1, ttt_norm_weight, ttt_norm_bias, ttt_lr_weight, ttt_lr_bias, learnable_token_idx, post_norm_weight, post_norm_bias):
            Bb, Ll, _ = hidden_states.shape
            NM = Ll // K

            def proj_heads(w):
                return (hidden_states @ w.T).reshape(Bb, Ll, NH, HD).transpose(0, 2, 1, 3)
            XQ = proj_heads(q_w).reshape(Bb, NH, NM, K, HD)
            XK = proj_heads(k_w).reshape(Bb, NH, NM, K, HD)
            XV = proj_heads(v_w).reshape(Bb, NH, NM, K, HD)
            X = hidden_states.reshape(Bb, NM, K, HS)
            ttt_lr = jnp.einsum('bnkc,hdc->bhnkd', X, ttt_lr_weight) + ttt_lr_bias.reshape(1, NH, 1, 1, 1)
            ttt_lr_eta = jax.nn.sigmoid(ttt_lr).transpose(0, 1, 2, 4, 3) / HD
            token_idx = jnp.clip(1.0 / jnp.arange(1, K + 1, dtype=jnp.float32) + learnable_token_idx, 0.0, None)
            eta = token_idx.reshape(1, 1, 1, K, 1) * ttt_lr_eta
            ln_w = ttt_norm_weight.reshape(NH, 1, HD)
            ln_b = ttt_norm_bias.reshape(NH, 1, HD)

            def step(carry, x):
                W1_s, b1_s = carry
                xq, xk, xv, eta_mb = x
                Z1 = xk @ W1_s + b1_s
                grad = _ln_fused_l2_bwd(Z1, xv - xk, ln_w, ln_b)
                Attn1 = jnp.tril(xq @ xk.swapaxes(-1, -2))
                b1_bar = b1_s - jnp.tril(eta_mb) @ grad
                Z1_bar = xq @ W1_s - eta_mb * Attn1 @ grad + b1_bar
                last_eta = eta_mb[:, :, -1, :, None]
                W1_new = W1_s - (last_eta * xk).swapaxes(-1, -2) @ grad
                b1_new = b1_s - jnp.sum(last_eta * grad, axis=-2, keepdims=True)
                out = xq + _ln(Z1_bar, ln_w, ln_b)
                return ((W1_new, b1_new), out)
            init = (jnp.tile(W1[None], (Bb, 1, 1, 1)), jnp.tile(b1[None], (Bb, 1, 1, 1)))
            xs = (XQ.transpose(2, 0, 1, 3, 4), XK.transpose(2, 0, 1, 3, 4), XV.transpose(2, 0, 1, 3, 4), eta.transpose(2, 0, 1, 3, 4))
            _, ys = jax.lax.scan(step, init, xs)
            out = ys.transpose(1, 0, 3, 2, 4).reshape(Bb, Ll, HS)
            out = _ln(out, post_norm_weight, post_norm_bias)
            return out @ o_w.T
        del position_ids
        return _forward(hidden_states, q_w, k_w, v_w, o_w, W1, b1, ttt_norm_weight, ttt_norm_bias, ttt_lr_weight, ttt_lr_bias, learnable_token_idx, post_norm_weight, post_norm_bias)

    def _L0_ffn_ref(hidden_states, router_gate, expert_gate_up, expert_down):
        import jax, jax.numpy as jnp
        import numpy as np
        NUM_EXPERTS = 8
        TOP_K = 2
        MODEL_DIM = 256
        INTER_DIM = 128
        GATE_SCALE = 1.0
        UP_SCALE = 0.0
        orig_shape = hidden_states.shape
        hs = hidden_states.reshape(-1, orig_shape[-1])
        T = hs.shape[0]
        logits = hs @ router_gate.T
        probs = jax.nn.softmax(logits.astype(jnp.float32), axis=-1)
        topk_scores, topk_idx = jax.lax.top_k(probs, TOP_K)
        topk_scores = topk_scores / jnp.sum(topk_scores, axis=-1, keepdims=True)
        scores_f = topk_scores.T.reshape(-1).astype(hs.dtype)
        ids_f = topk_idx.T.reshape(-1)
        order = jnp.argsort(ids_f)
        sorted_ids = ids_f[order]
        scores_sorted = scores_f[order]
        token_slots = order % T
        x = hs[token_slots]
        inter = jnp.zeros((x.shape[0], 2 * INTER_DIM), x.dtype)
        for e in range(NUM_EXPERTS):
            m = (sorted_ids == e)[:, None]
            inter = inter + jnp.where(m, x, 0) @ expert_gate_up[e]
        gate = inter[..., 0::2]
        up = inter[..., 1::2]
        h = (up + UP_SCALE) * jax.nn.silu(gate * GATE_SCALE)
        out_rows = jnp.zeros((x.shape[0], MODEL_DIM), x.dtype)
        for e in range(NUM_EXPERTS):
            m = (sorted_ids == e)[:, None]
            out_rows = out_rows + jnp.where(m, h, 0) @ expert_down[e]
        out = jnp.zeros_like(hs).at[token_slots].add(out_rows * scores_sorted[:, None])
        return out.reshape(orig_shape)
    x = L0_attn_hidden_states
    xn = _layernorm(x, axis=-1)
    s = _L0_attn_ref(xn, L0_attn_position_ids, L0_attn_q_w, L0_attn_k_w, L0_attn_v_w, L0_attn_o_w, L0_attn_W1, L0_attn_b1, L0_attn_ttt_norm_weight, L0_attn_ttt_norm_bias, L0_attn_ttt_lr_weight, L0_attn_ttt_lr_bias, L0_attn_learnable_token_idx, L0_attn_post_norm_weight, L0_attn_post_norm_bias)
    g = _silu(_L0_ffn_ref(xn, L0_ffn_router_gate, L0_ffn_expert_gate_up, L0_ffn_expert_down))
    x = x + s * g
    return x

_drawn_inputs = setup_inputs


def setup_inputs(seed=0):
    import zlib

    import numpy as np

    out = dict(_drawn_inputs(seed))
    spreads = {'L0_attn_b1': (0.0, 0.8),
     'L0_attn_ttt_norm_weight': (1.0, 0.6),
     'L0_attn_ttt_norm_bias': (0.0, 0.8),
     'L0_attn_ttt_lr_bias': (0.0, 0.8),
     'L0_attn_learnable_token_idx': (0.0, 0.8),
     'L0_attn_post_norm_weight': (1.0, 0.6),
     'L0_attn_post_norm_bias': (0.0, 0.8)}
    factors = {'L0_attn_q_w': 8.0,
     'L0_attn_k_w': 8.0,
     'L0_attn_v_w': 8.0,
     'L0_attn_o_w': 8.0,
     'L0_attn_W1': 8.0,
     'L0_attn_ttt_lr_weight': 8.0,
     'L0_ffn_router_gate': 8.0,
     'L0_ffn_expert_gate_up': 8.0,
     'L0_ffn_expert_down': 8.0}
    for name, (base, spread) in spreads.items():
        noise = np.random.default_rng([zlib.crc32(name.encode()), seed]).standard_normal(out[name].shape)
        drawn = base * np.exp(spread * noise) if base else spread * noise
        out[name] = jnp.asarray(drawn.astype(out[name].dtype))
    for name, factor in factors.items():
        out[name] = (out[name] * factor).astype(out[name].dtype)
    return out
```

```python
import concourse.bass as bass
from concourse import mybir
from contextlib import ExitStack

F32 = mybir.dt.float32
U32 = mybir.dt.uint32
ALU = mybir.AluOpType
ACT = mybir.ActivationFunctionType
AX = mybir.AxisListType

P = 128
B, L, HS = 4, 256, 256
NH, HD, K = 32, 8, 16
NG = 8
GT = L // NG
KC = HS // P
HH = P // HD
C1 = HD + 1
NE, NI = 8, 128
NF = NG
WSAVE = 16 * (B * KC + B)
EPS_IN, EPS = 1e-5, 1e-6


def build(nc, x_bt_d, wk_d, wv_d, wq_d, wo_d, wlr_d, wrt_d, gup_d, down_d, pair_d, rows_d, lti_d,
          post_d, ident_d, hmask_d, mask_tok_d, mask_last_d, sel_d, iota_d, inv_d, out_d):
    bd_d = nc.dram_tensor("w_blocks", [B * KC, P, P], F32, kind="Internal")

    with ExitStack() as ctx:
        def sb(name, shape, dt=F32):
            return ctx.enter_context(nc.sbuf_tensor(name, shape, dt))

        def sem(name):
            return ctx.enter_context(nc.semaphore(name))

        bank = [ctx.enter_context(nc.psum_tensor(f"bank{i}", [P, 512], F32)) for i in range(8)]

        x_bt = sb("x_bt", [P, NG, HS])
        xn = sb("xn", [P, NG, HS])
        xnT = sb("xnT", [P, KC, NG, P])
        wk = sb("wk", [P, KC, HS])
        wv = sb("wv", [P, KC, HS])
        wq = sb("wq", [P, KC, HS])
        wo = sb("wo", [P, KC, HS])
        wlr = sb("wlr", [P, KC, NH])
        wrt = sb("wrt", [P, KC, NE])
        gup = sb("gup", [P, KC, NE, 2 * NI])
        down = sb("down", [P, NE, HS])
        pairp = sb("pairp", [P, 2 * HD + C1 * HD + 1])
        rows = sb("rows", [P, 2, HS])
        lti = sb("lti", [P, K])
        post = sb("post", [P, 2, KC])
        ident = sb("ident", [P, P])
        hmask = sb("hmask", [P, 4])
        mask_tok = sb("mask_tok", [P, GT])
        mask_last = sb("mask_last", [P, GT])
        sel = sb("sel", [4, P])
        iota = sb("iota", [P, NE])
        inv = sb("inv", [P, K])
        ones_row = sb("ones_row", [1, P])
        eps_in = sb("eps_in", [P, 1])
        eps = sb("eps", [P, 1])

        stats = sb("stats", [P, NG, 6])
        mv = sb("mv", [P, NG, 2])
        std_in = sb("std_in", [P, NG])
        rstd_in = sb("rstd_in", [P, NG])
        wt = sb("wt", [P, KC, HS])
        wtree = sb("wtree", [P, KC * HS // 2])
        grow = sb("grow", [P, HS])
        growtree = sb("growtree", [P, HS // 2])
        tok = sb("tok", [P, K])
        ntok = sb("ntok", [P, 1])
        mask = sb("mask", [P, GT])
        mask2 = sb("mask2", [P, GT])
        g2 = sb("g2", [P, HD])

        xkT = sb("xkT", [P, KC, NG, P])
        xqT = sb("xqT", [P, KC, B, L])
        xqm = sb("xqm", [P, 2, KC, B, 4, GT])
        KP = sb("KP", [P, NG * C1 * GT])
        QP = sb("QP", [P, NG * HD * GT])
        eta = sb("eta", [P, NG, GT])
        sig = sb("sig", [P, NG * GT])

        W = sb("W", [P, 2, C1 * HD])
        wmean = sb("wmean", [P, C1])
        pr1 = sb("pr1", [P, HD * K * C1])
        pr2 = sb("pr2", [P, C1 * HD * K])
        T = sb("T", [P, 5, HD * K])
        S = sb("S", [P, 4, K])
        sxx = sb("sxx", [P, K])
        sd = sb("sd", [P, K])
        rr = sb("rr", [P, 3, K])
        cf = sb("cf", [P, 4, K])
        hb = sb("hb", [P, 5, HD * K])
        sgb = sb("sgb", [P, HD, GT])
        sgT = sb("sgT", [P, HD, NH])
        sgpad = sb("sgpad", [P, 2, NH, B, HD])
        dW = sb("dW", [P, C1 * HD])
        A = sb("A", [P, 2, 4, 2 * 4 * GT])
        bdw = sb("bdw", [P, 2, B * KC, P])
        biasr = sb("biasr", [4, 2, NH * B * HD])

        mx = sb("mx", [P, NF, 8])
        mi = sb("mi", [P, NF, 8], U32)
        mif = sb("mif", [P, NF, 2])
        gap = sb("gap", [P, NF])
        s12 = sb("s12", [P, 2, NF])
        oh = sb("oh", [P, 2, NF, NE])
        wexp = sb("wexp", [P, NF, NE])
        gate = sb("gate", [P, 2, 2, NI])
        upw = sb("upw", [P, 2, 2, NI])
        hh = sb("hh", [P, 2, 2, NI])
        hT = sb("hT", [P, 2, 2, P])
        G = sb("G", [P, NF, HS])

        xqb = sb("xqb", [P, 2, NH, B, HD])
        zc = sb("zc", [P, 2, NH * B * HD])
        yn = xn[:, :, :].rearrange("p (u b) c -> p u b c", u=2)
        zsq = sb("zsq", [P, NH * B * HD])
        zv = sb("zv", [P, NH * B])
        zs = sb("zs", [P, NH * B])
        zr = sb("zr", [P, NH * B])
        o = sb("o", [P, NH * B * HD])
        ostat = sb("ostat", [P, B, 6])
        omv = sb("omv", [P, B, 2])
        osd = sb("osd", [P, B])
        ors = sb("ors", [P, B])
        yT = sb("yT", [P, KC, 4, P])
        res = sb("res", [P, 2, HS])

        s_x = [sem(f"s_x{i}") for i in range(4)]
        s_par = sem("s_par")
        s_wkv = sem("s_wkv")
        s_wq = sem("s_wq")
        s_wexp = sem("s_wexp")
        s_late = sem("s_late")
        s_pool = sem("s_pool")
        s_wt = sem("s_wt")
        s_dve0 = sem("s_dve0")
        s_var = sem("s_var")
        s_stdin = sem("s_stdin")
        s_xn = sem("s_xn")
        s_xnT = sem("s_xnT")
        s_xnTa = sem("s_xnTa")
        s_xnTv = sem("s_xnTv")
        s_kq = sem("s_kq")
        s_kqc = sem("s_kqc")
        s_eta = sem("s_eta")
        s_etaT = sem("s_etaT")
        s_sig = sem("s_sig")
        s_pair = sem("s_pair")
        s_pairT = sem("s_pairT")
        s_tq = sem("s_tq")
        s_tqc = sem("s_tqc")
        s_xqb = sem("s_xqb")
        s_route = sem("s_route")
        s_gap = sem("s_gap")
        s_s12 = sem("s_s12")
        s_wx = sem("s_wx")
        s_rdve = sem("s_rdve")
        s_xqm = sem("s_xqm")
        s_sc = sem("s_sc")
        s_mask = sem("s_mask")
        s_chain = sem("s_chain")
        s_sxx = sem("s_sxx")
        s_sd = sem("s_sd")
        s_sg = sem("s_sg")
        s_w = sem("s_w")
        s_wsave = sem("s_wsave")
        s_bdz = sem("s_bdz")
        s_bd = sem("s_bd")
        s_sgT = sem("s_sgT")
        s_sgp = sem("s_sgp")
        s_z0 = sem("s_z0")
        s_z = sem("s_z")
        s_zh = sem("s_zh")
        s_zc = sem("s_zc")
        s_gu = sem("s_gu")
        s_gact = sem("s_gact")
        s_h = sem("s_h")
        s_hTp = sem("s_hTp")
        s_hT = sem("s_hT")
        s_y = sem("s_y")
        s_g = sem("s_g")
        s_zv = sem("s_zv")
        s_zs = sem("s_zs")
        s_post = sem("s_post")
        s_ov = sem("s_ov")
        s_os = sem("s_os")
        s_yn = sem("s_yn")
        s_yTp = sem("s_yTp")
        s_yT = sem("s_yT")
        s_o = sem("s_o")
        s_res = sem("s_res")
        s_res1 = sem("s_res1")
        s_out = [sem(f"s_out{i}") for i in range(2)]

        block = ctx.enter_context(nc.Block())

        def head_at(h):
            hf, r = divmod(h, HH)
            return r // 4, hf * 4 + r % 4

        @block.sync
        def _(sp):
            for i in range(4):
                sp.dma_start(x_bt[:, 2 * i:2 * i + 2, :], x_bt_d[:, 2 * i:2 * i + 2, :]).then_inc(s_x[i], 16)
            sp.dma_start(wk[:, :, :], wk_d).then_inc(s_wkv, 16)
            sp.dma_start(wv[:, :, :], wv_d).then_inc(s_wkv, 16)
            sp.dma_start(wq[:, :, :], wq_d).then_inc(s_wq, 16)
            sp.dma_start(wlr[:, :, :], wlr_d).then_inc(s_wq, 16)
            sp.dma_start(wrt[:, :, :], wrt_d).then_inc(s_wq, 16)
            sp.wait_ge(s_bdz, 1)
            sp.dma_start(bd_d.ap().rearrange("g p c -> p g c"), bdw[:, 0, :, :]).then_inc(s_bd, 16)
            sp.dma_start(gup[:, :, :, :], gup_d).then_inc(s_wexp, 16)
            sp.dma_start(down[:, :, :], down_d).then_inc(s_wexp, 16)
            sp.dma_start(wo[:, :, :], wo_d).then_inc(s_late, 16)
            sp.dma_start(post[:, :, :], post_d).then_inc(s_late, 16)
            sp.wait_ge(s_bd, 16)
            for j in range(NG):
                sp.wait_ge(s_w, 2 * j + 1)
                sp.wait_ge(s_bd, 16 * (j + 1))
                for g in range(B * KC):
                    sp.dma_start(bass.AP(bd_d, g * P * P, [[HD * P + HD, HH], [P, HD], [1, HD]]),
                                 W[g * HH:g * HH + HH, 0, 0:HD * HD].rearrange("h (c d) -> h c d", d=HD)
                                 ).then_inc(s_wsave, 16)
                if j == 4:
                    sp.wait_ge(s_zh, 1)
                for b in range(B):
                    sp.dma_start(biasr[j % 4:j % 4 + 1, j // 4, :].rearrange("p (h b d) -> p b h d", b=B, d=HD)[:, b],
                                 W[b * NH:b * NH + NH, 0, HD * HD:]).then_inc(s_wsave, 16)
                sp.wait_ge(s_wsave, WSAVE * (j + 1))
                if j >= 2:
                    sp.wait_ge(s_z0, j - 1)
                sp.dma_start(bdw[:, j % 2, :, :], bd_d.ap().rearrange("g p c -> p g c")).then_inc(s_bd, 16)
            for f in range(NF):
                sp.wait_ge(s_res, f + 1)
                sp.dma_start(out_d[:, f, :], res[:, f % 2, :]).then_inc(s_out[f % 2], 16)
            for i in range(2):
                sp.wait_ge(s_out[i], 16 * NF // 2)

        @block.gpsimd
        def _(pool):
            pool.memset(bdw[:, 0, :, :], 0.0).then_inc(s_bdz, 1)
            pool.memset(sgpad[:, :, :, :, :], 0.0).then_inc(s_sgp, 1)
            kp4 = KP[:, :].rearrange("p (j c t) -> p j c t", j=NG, c=C1)
            pool.memset(kp4[:, :, HD, :], 1.0).then_inc(s_pool, 1)
            pool.memset(ones_row[:, :], 1.0).then_inc(s_pool, 1)
            pool.wait_ge(s_wkv, 32)
            pool.wait_ge(s_par, 16 * 10)
            n = [2]

            def link(ins):
                n[0] += 1
                ins.then_inc(s_pool, 1)
                pool.wait_ge(s_pool, n[0])

            def bc_rows(a):
                return a.unsqueeze(1).broadcast_to([P, KC, HS])

            def centre(full, tree, m):
                v = full.rearrange("p (m d) -> p m d", d=HD)
                t4 = tree.rearrange("p (m d) -> p m d", d=4)
                link(pool.tensor_tensor(t4, v[:, :, 0:4], v[:, :, 4:8], ALU.add))
                link(pool.tensor_tensor(t4[:, :, 0:2], t4[:, :, 0:2], t4[:, :, 2:4], ALU.add))
                link(pool.tensor_tensor(t4[:, :, 0:1], t4[:, :, 0:1], t4[:, :, 1:2], ALU.add))
                link(pool.tensor_scalar(t4[:, :, 0:1], t4[:, :, 0:1], -1.0 / HD, 0.0, ALU.mult, ALU.add))
                return pool.tensor_tensor(v, v, t4[:, :, 0:1].broadcast_to([P, m, HD]), ALU.add)

            link(pool.tensor_tensor(wt[:, :, :], wk[:, :, :], wv[:, :, :], ALU.subtract))
            link(pool.tensor_tensor(wt[:, :, :], wt[:, :, :], bc_rows(rows[:, 0, :]), ALU.mult))
            link(centre(wt[:, :, :].rearrange("p a b -> p (a b)"), wtree[:, :], KC * NH))
            link(pool.tensor_tensor(grow[:, :], rows[:, 0, :], rows[:, 1, :], ALU.mult))
            centre(grow[:, :], growtree[:, :], NH).then_inc(s_wt, 1)
            pool.wait_ge(s_tqc, 4)
            bb = rows[:, 1, :].rearrange("p (h d) -> p h d", d=HD).unsqueeze(2).broadcast_to([P, NH, B, HD])
            for u in range(2):
                pool.tensor_tensor(xqb[:, u, :, :, :], xqb[:, u, :, :, :], bb, ALU.add).then_inc(s_xqb, 1)
            for i in range(NF * 4):
                pool.wait_ge(s_gact, 3 * (i + 1))
                if i >= 2:
                    pool.wait_ge(s_hTp, i - 1)
                pool.tensor_tensor(hh[:, i % 2, :, :], gate[:, i % 2, :, :], upw[:, i % 2, :, :],
                                   ALU.mult).then_inc(s_h, 1)

        @block.scalar
        def _(act):
            pl = [(pairp, pair_d), (rows, rows_d), (lti, lti_d), (ident, ident_d), (hmask, hmask_d),
                  (mask_tok, mask_tok_d), (mask_last, mask_last_d), (sel, sel_d), (iota, iota_d), (inv, inv_d)]
            for t, d in pl:
                act.dma_start(t[:], d).then_inc(s_par, 16)
            act.wait_ge(s_dve0, 2)
            act.wait_ge(s_var, 1)
            act.activation(std_in[:, :], mv[:, :, 1], ACT.Sqrt, bias=eps_in[:, 0:1]).then_inc(s_stdin, 1)
            for i in (0, 2):
                act.wait_ge(s_xnT, i + 1)
                act.copy(xnT[:, i // 2, 0:4, :].rearrange("p j t -> p (j t)"), bank[4 + i][:, :]).then_inc(s_xnTa, 1)
            for i in range(8):
                act.wait_ge(s_kq, i + 1)
                hf, u = i % 2, i % 4 // 2
                if i < 4:
                    act.copy(xkT[:, hf, 4 * u:4 * u + 4, :].rearrange("p j t -> p (j t)"),
                             bank[i % 4][:, :]).then_inc(s_kqc, 1)
                else:
                    act.copy(xqT[:, hf, :, P * u:P * u + P].rearrange("p b (j t) -> p j b t", t=GT),
                             bank[i % 4][:, :].rearrange("p (j b t) -> p j b t", j=4, b=B)).then_inc(s_kqc, 1)
                if i == 3:
                    act.wait_ge(s_etaT, 1)
                    act.activation(sig[:, :], eta[:, :, :].rearrange("p j t -> p (j t)"), ACT.Sigmoid,
                                   bias=pairp[:, 2 * HD + C1 * HD:]).then_inc(s_sig, 1)

            def masked_queries(j):
                act.wait_ge(s_kqc, 8)
                if j >= 2:
                    act.wait_ge(s_sc, 4 * (j - 1))
                for h in range(4):
                    act.activation(xqm[:, j % 2, :, :, h, :],
                                   xqT[:, :, :, GT * j:GT * j + GT],
                                   ACT.Copy, scale=hmask[:, h:h + 1]).then_inc(s_xqm, 1)

            def query_rows():
                for i in range(4):
                    act.wait_ge(s_tq, i + 1)
                    u, hf = divmod(i, 2)
                    act.copy(xqb[:, u, hf * HH:(hf + 1) * HH, :, :],
                             bank[4 + i % 2][:, :].rearrange("p (b h d) -> p h b d", b=B, d=HD)).then_inc(s_tqc, 1)

            def std(n):
                act.wait_ge(s_sxx, n + 1)
                act.activation(sd[:, :], sxx[:, :], ACT.Sqrt, bias=eps[:, 0:1], scale=1.0 / HD).then_inc(s_sd, 1)

            def pad_grads(j):
                act.wait_ge(s_sgT, j + 1)
                if j == 0:
                    act.wait_ge(s_sgp, 1)
                if j >= 2:
                    act.wait_ge(s_z, j - 1)
                for b in range(B):
                    q = slice(32 * b, 32 * b + 32)
                    act.copy(sgpad[q, j % 2, :, b, :], sgT[q, :, :].rearrange("p d h -> p h d")).then_inc(s_sgp, 1)

            def expert_pair(f, e):
                i = 4 * f + e
                bk = bank[4 + i % 2][:, :].rearrange("p (e g i) -> p e g i", e=2, g=2)
                act.wait_ge(s_gu, i + 1)
                if i >= 2:
                    act.wait_ge(s_h, i - 1)
                act.activation(gate[:, i % 2, :, :], bk[:, :, 0, :], ACT.Silu).then_inc(s_gact, 1)
                for r in range(2):
                    act.activation(upw[:, i % 2, r, :], bk[:, r, 1, :], ACT.Copy,
                                   scale=wexp[:, f, 2 * e + r:2 * e + r + 1]).then_inc(s_gact, 1)

            def hidden_out(i):
                act.wait_ge(s_hTp, i + 1)
                if i >= 2:
                    act.wait_ge(s_y, i - 1)
                act.copy(hT[:, i % 2, :, :].rearrange("p e t -> p (e t)"), bank[6][:, 0:256]).then_inc(s_hT, 1)

            def half_out(u):
                act.wait_ge(s_zh, u + 1)
                for k in range(2):
                    act.copy(zc[:, u, 512 * k:512 * k + 512], bank[k][:, :]).then_inc(s_zc, 1)

            masked_queries(0)
            query_rows()
            act.wait_ge(s_gap, 1)
            act.activation(s12[:, 0, :], gap[:, :], ACT.Sigmoid).then_inc(s_s12, 1)
            act.activation(s12[:, 1, :], gap[:, :], ACT.Sigmoid, scale=-1.0).then_inc(s_s12, 1)
            act.wait_ge(s_wx, 1)
            for j in range(NG):
                if j + 1 < NG:
                    masked_queries(j + 1)
                std(2 * j)
                for e in range(4):
                    expert_pair(j, e)
                    hidden_out(4 * j + e)
                    if e == 2:
                        std(2 * j + 1)
                act.wait_ge(s_y, 4 * j + 4)
                act.activation(G[:, j, :], bank[7][:, 0:HS], ACT.Silu).then_inc(s_g, 1)
                pad_grads(j)
                if j % 4 == 3:
                    half_out(j // 4)
            for u in range(2):
                act.wait_ge(s_zv, u + 1)
                act.activation(zs[:, :], zv[:, :], ACT.Sqrt, bias=eps[:, 0:1], scale=1.0 / HD).then_inc(s_zs, 1)
                act.wait_ge(s_ov, u + 1)
                act.activation(osd[:, :], omv[:, :, 1], ACT.Sqrt, bias=eps[:, 0:1]).then_inc(s_os, 1)
                if u == 1:
                    act.wait_ge(s_o, 4)
                for b in range(B):
                    i = 4 * u + b
                    act.wait_ge(s_yTp, i + 1)
                    for k in range(KC):
                        act.activation(yT[:, k, :, GT * b:GT * b + GT],
                                       bank[2 + i % 2][:, P * k:P * k + P].rearrange("p (j t) -> p j t", t=GT),
                                       ACT.Identity, scale=post[:, 0, k:k + 1],
                                       bias=post[:, 1, k:k + 1]).then_inc(s_yT, 1)

        @block.vector
        def _(v):
            n0 = [0]

            def link(ins, semaphore=s_dve0, count=n0):
                count[0] += 1
                ins.then_inc(semaphore, 1)
                v.wait_ge(semaphore, count[0])

            v.wait_ge(s_par, 16 * 10)
            link(v.memset(eps_in[:, :], EPS_IN))
            link(v.memset(eps[:, :], EPS))
            for j in range(NG):
                v.wait_ge(s_x[j // 2], 16)
                ins = v.bn_stats(stats[:, j, :], x_bt[:, j, :])
                if j == NG - 1:
                    link(ins)
            for j in range(NG):
                ins = v.bn_aggr(mv[:, j, :], stats[:, j, :])
            ins.then_inc(s_var, 1)
            gam, bet = pairp[:, 0:HD], pairp[:, HD:2 * HD]
            link(v.tensor_tensor(g2[:, :], gam, gam, ALU.mult))
            link(v.tensor_tensor(tok[:, :], inv[:, :], lti[:, :], ALU.add))
            link(v.tensor_scalar(tok[:, :], tok[:, :], 0.0, None, ALU.max))
            link(v.tensor_scalar(ntok[:, :], tok[:, K - 1:K], -1.0 / HD, None, ALU.mult))
            link(v.tensor_tensor(mask[:, :].rearrange("p (m t) -> p m t", t=K),
                                 mask_tok[:, :].rearrange("p (m t) -> p m t", t=K),
                                 tok[:, :].unsqueeze(1).broadcast_to([P, 2, K]), ALU.mult))
            link(v.tensor_scalar(mask2[:, :], mask_last[:, :], tok[:, K - 1:K], None, ALU.mult))
            link(v.tensor_tensor(mask[:, :], mask[:, :], mask2[:, :], ALU.add))
            w0 = pairp[:, 2 * HD:2 * HD + C1 * HD].rearrange("p (c d) -> p c d", d=HD)
            link(v.tensor_reduce(wmean[:, :], w0, AX.X, ALU.add))
            link(v.tensor_scalar(wmean[:, :], wmean[:, :], -1.0 / HD, None, ALU.mult))
            v.tensor_tensor(W[:, 0, :].rearrange("p (c d) -> p c d", d=HD), w0,
                            wmean[:, :].unsqueeze(2).broadcast_to([P, C1, HD]), ALU.add).then_inc(s_w, 1)
            v.wait_ge(s_stdin, 1)
            link(v.reciprocal(rstd_in[:, :], std_in[:, :]))
            for j in range(NG):
                v.tensor_scalar(xn[:, j, :], x_bt[:, j, :], mv[:, j, 0:1], rstd_in[:, j:j + 1],
                                ALU.subtract, ALU.mult).then_inc(s_xn, 1)
            for i in (1, 3):
                v.wait_ge(s_xnT, i + 1)
                v.tensor_copy(xnT[:, i // 2, 4:8, :].rearrange("p j t -> p (j t)"), bank[4 + i][:, :]).then_inc(s_xnTv, 1)
            v.wait_ge(s_eta, 1)
            v.transpose(eta[:, :, :].rearrange("p j t -> p (j t)"), bank[4][:, 0:256]).then_inc(s_etaT, 1)
            for j in range(NG):
                bk = bank[5 + j % 3]
                v.wait_ge(s_pair, j + 1)
                kdst = KP[:, j * C1 * GT:(j * C1 + HD) * GT].rearrange("p (c t) -> p c t", c=HD)
                v.transpose(kdst, bk[:, 0:256].rearrange("p (h c) -> p c h", c=HD))
                v.transpose(QP[:, j * HD * GT:(j + 1) * HD * GT].rearrange("p (c t) -> p c t", c=HD),
                            bk[:, 256:512].rearrange("p (h c) -> p c h", c=HD)).then_inc(s_pairT, 1)
            r0 = [0]
            v.wait_ge(s_route, 1)
            for f in range(NF):
                ins = v.max(mx[:, f, :], bank[7][:, f * NE:(f + 1) * NE])
            link(ins, s_rdve, r0)
            for f in range(NF):
                ins = v.max_index(mi[:, f, :], mx[:, f, :], bank[7][:, f * NE:(f + 1) * NE])
            link(ins, s_rdve, r0)
            v.tensor_tensor(gap[:, :], mx[:, :, 0], mx[:, :, 1], ALU.subtract).then_inc(s_gap, 1)
            link(v.tensor_copy(mif[:, :, :], mi[:, :, 0:2]), s_rdve, r0)
            for k in range(2):
                link(v.tensor_tensor(oh[:, k, :, :], iota[:, :].unsqueeze(1).broadcast_to([P, NF, NE]),
                                     mif[:, :, k:k + 1].broadcast_to([P, NF, NE]), ALU.is_equal), s_rdve, r0)
            v.wait_ge(s_s12, 2)
            for k in range(2):
                link(v.tensor_tensor(oh[:, k, :, :], oh[:, k, :, :],
                                     s12[:, k, :].unsqueeze(2).broadcast_to([P, NF, NE]), ALU.mult), s_rdve, r0)
            v.tensor_tensor(wexp[:, :, :], oh[:, 0, :, :], oh[:, 1, :, :], ALU.add).then_inc(s_wx, 1)

            mask_bc = mask[:, :].unsqueeze(1).broadcast_to([P, 8, GT])

            def masks(j, ring, q):
                v.wait_ge(s_sc, 4 * j + q + 1)
                v.scalar_tensor_tensor(
                    out=A[:, ring, q, :].rearrange("p (h t) -> p h t", t=GT),
                    in0=bank[2 + q % 2][:, 0:256].rearrange("p (h t) -> p h t", t=GT), scalar=1.0, in1=mask_bc,
                    op0=ALU.add, op1=ALU.mult).then_inc(s_mask, 1)

            OPS = 18

            def minibatch(j, m, fill):
                n = j * 2 + m
                Wn = W[:, m, :]
                kp = KP[:, bass.ds(j * (C1 * GT), C1 * GT)].rearrange("p (c t) -> p c t", c=C1)[:, :, K * m:K * m + K]
                qn = QP[:, bass.ds(j * (HD * GT), HD * GT)].rearrange("p (d t) -> p d t", d=HD)[:, :, K * m:K * m + K]
                sg_n = sig[:, bass.ds(j * GT + K * m, K)]
                done = lambda k: v.wait_ge(s_chain, n * OPS + k)
                sl = lambda i: T[:, i, :].rearrange("p (d t) -> p d t", d=HD)
                b3 = lambda a: a.unsqueeze(1).broadcast_to([P, HD, K])
                x, u, pq, ux, xx = (sl(i) for i in range(5))

                v.wait_ge(s_w, n + 1)
                v.tensor_tensor(pr1[:, :].rearrange("p (d t c) -> p d t c", d=HD, t=K),
                                kp.rearrange("p c t -> p t c").unsqueeze(1).broadcast_to([P, HD, K, C1]),
                                Wn.rearrange("p (c d) -> p d c", d=HD).unsqueeze(2).broadcast_to([P, HD, K, C1]),
                                ALU.mult).then_inc(s_chain, 1)
                fill(0)
                done(1)
                v.tensor_reduce(T[:, 0, :], pr1[:, :].rearrange("p (a c) -> p a c", c=C1), AX.X,
                                ALU.add).then_inc(s_chain, 1)
                done(2)
                v.tensor_tensor(xx, x, x, ALU.mult).then_inc(s_chain, 1)
                v.tensor_tensor(u, x, g2[:, :].unsqueeze(2).broadcast_to([P, HD, K]), ALU.mult).then_inc(s_chain, 1)
                done(3)
                v.tensor_reduce(sxx[:, :], xx.rearrange("p d t -> p t d"), AX.X, ALU.add).then_inc(s_sxx, 1)
                v.tensor_tensor(pq, x, qn, ALU.mult).then_inc(s_chain, 1)
                done(4)
                v.tensor_tensor(ux, x, u, ALU.mult).then_inc(s_chain, 1)
                done(6)
                v.tensor_reduce(S[:, 1:4, :], T[:, 1:4, :].rearrange("p k (d t) -> p k t d", d=HD), AX.X,
                                ALU.add).then_inc(s_chain, 1)
                v.wait_ge(s_sd, n + 1)
                v.reciprocal(rr[:, 0, :], sd[:, :]).then_inc(s_chain, 1)
                done(8)
                r = rr[:, 0, :]
                v.tensor_tensor(cf[:, 3, :], r, sg_n, ALU.mult).then_inc(s_chain, 1)
                v.tensor_tensor(rr[:, 1, :], r, S[:, 3, :], ALU.mult).then_inc(s_chain, 1)
                done(9)
                v.tensor_tensor(cf[:, 1, :], r, cf[:, 3, :], ALU.mult).then_inc(s_chain, 1)
                done(10)
                v.tensor_tensor(rr[:, 2, :], rr[:, 1, :], S[:, 2, :], ALU.add).then_inc(s_chain, 1)
                v.tensor_tensor(hb[:, 2, :].rearrange("p (d t) -> p d t", d=HD), qn, b3(cf[:, 3, :]),
                                ALU.mult).then_inc(s_chain, 1)
                done(12)
                v.tensor_tensor(S[:, 0, :], rr[:, 2, :], r, ALU.mult).then_inc(s_chain, 1)
                done(14)
                v.scalar_tensor_tensor(out=cf[:, 0:3:2, :], in0=S[:, 0:2, :], scalar=-1.0 / HD,
                                       in1=cf[:, 1:2, :].broadcast_to([P, 2, K]),
                                       op0=ALU.mult, op1=ALU.mult).then_inc(s_chain, 1)
                done(15)
                v.tensor_tensor(hb[:, 0:2, :].rearrange("p k (d t) -> p k d t", d=HD),
                                T[:, 0:2, :].rearrange("p k (d t) -> p k d t", d=HD),
                                cf[:, 0:2, :].unsqueeze(2).broadcast_to([P, 2, HD, K]), ALU.mult).then_inc(s_chain, 1)
                hv = lambda i: hb[:, i, :].rearrange("p (d t) -> p d t", d=HD)
                v.tensor_tensor(hv(3), hv(2), b3(cf[:, 2, :]), ALU.add).then_inc(s_chain, 1)
                done(16)
                v.tensor_tensor(hv(4), hv(0), hv(1), ALU.add).then_inc(s_chain, 1)
                done(18)
                sg = sgb[:, :, K * m:K * m + K]
                v.tensor_tensor(sg, hv(4), hv(3), ALU.add).then_inc(s_sg, 1)
                v.wait_ge(s_sg, 3 * n + 1)
                v.tensor_tensor(pr2[:, :].rearrange("p (c d t) -> p c d t", c=C1, d=HD),
                                kp.unsqueeze(2).broadcast_to([P, C1, HD, K]),
                                sg.unsqueeze(1).broadcast_to([P, C1, HD, K]), ALU.mult).then_inc(s_sg, 1)
                fill(1)
                v.wait_ge(s_sg, 3 * n + 2)
                v.tensor_reduce(dW[:, :], pr2[:, :].rearrange("p (a t) -> p a t", t=K), AX.X,
                                ALU.add).then_inc(s_sg, 1)
                v.wait_ge(s_sg, 3 * n + 3)
                if m == 1:
                    v.wait_ge(s_wsave, WSAVE * (j + 1))
                v.scalar_tensor_tensor(out=W[:, 1 - m, :], in0=dW[:, :], scalar=ntok[:, 0:1], in1=Wn,
                                       op0=ALU.mult, op1=ALU.add).then_inc(s_w, 1)

            def group(j, ring, more):
                for m in range(2):
                    minibatch(j, m, (lambda i: masks(j + 1, 1 - ring, 2 * m + i)) if more else (lambda i: None))
                v.wait_ge(s_sgp, 4 * j + 1)
                v.transpose(sgT[:, :, :].rearrange("p d h -> p (d h)"),
                            sgb[:, :, :].rearrange("p d t -> p (d t)")).then_inc(s_sgT, 1)

            v.wait_ge(s_pairT, NG)
            v.wait_ge(s_sig, 1)
            v.wait_ge(s_pool, 1)
            for q in range(4):
                masks(0, 0, q)
            with v.Fori(0, NG - 2, 2) as j:
                group(j, 0, True)
                group(j + 1, 1, True)
            group(NG - 2, 0, True)
            group(NG - 1, 1, False)

            p0 = [0]
            for u in range(2):
                v.wait_ge(s_zc, 2 * (u + 1))
                z4 = zc[:, u, :]
                link(v.tensor_tensor(zsq[:, :], z4, z4, ALU.mult), s_post, p0)
                v.tensor_reduce(zv[:, :], zsq[:, :].rearrange("p (a d) -> p a d", d=HD), AX.X, ALU.add).then_inc(s_zv, 1)
                v.wait_ge(s_zs, u + 1)
                link(v.reciprocal(zr[:, :], zs[:, :]), s_post, p0)
                o3 = o[:, :].rearrange("p (a d) -> p a d", d=HD)
                link(v.tensor_tensor(o3, z4.rearrange("p (a d) -> p a d", d=HD),
                                     zr[:, :].unsqueeze(2).broadcast_to([P, NH * B, HD]), ALU.mult), s_post, p0)
                o4 = o[:, :].rearrange("p (h b d) -> p h b d", b=B, d=HD)
                link(v.tensor_tensor(o4, o4, rows[:, 0, :].rearrange("p (h d) -> p h d", d=HD).unsqueeze(2)
                                     .broadcast_to([P, NH, B, HD]), ALU.mult), s_post, p0)
                v.wait_ge(s_xqb, 2)
                link(v.tensor_tensor(o4, o4, xqb[:, u, :, :, :], ALU.add), s_post, p0)
                for b in range(B):
                    ins = v.bn_stats(ostat[:, b, :], o4[:, :, b, :])
                link(ins, s_post, p0)
                for b in range(B):
                    ins = v.bn_aggr(omv[:, b, :], ostat[:, b, :])
                ins.then_inc(s_ov, 1)
                v.wait_ge(s_os, u + 1)
                link(v.reciprocal(ors[:, :], osd[:, :]), s_post, p0)
                for b in range(B):
                    v.tensor_scalar(yn[:, u, b, :].rearrange("p (h d) -> p h d", d=HD), o4[:, :, b, :],
                                    omv[:, b, 0:1], ors[:, b:b + 1], ALU.subtract, ALU.mult).then_inc(s_yn, 1)
                for j in range(4 * u, 4 * u + 4):
                    v.wait_ge(s_o, j + 1)
                    v.wait_ge(s_g, NG)
                    if j >= 2:
                        v.wait_ge(s_out[j % 2], 16 * (j // 2))
                    v.tensor_tensor(res[:, j % 2, :], bank[4 + j % 2][:, 0:HS], G[:, j, :], ALU.mult).then_inc(s_res1, 1)
                    v.wait_ge(s_res1, j + 1)
                    v.tensor_tensor(res[:, j % 2, :], res[:, j % 2, :], x_bt[:, j, :], ALU.add).then_inc(s_res, 1)

        @block.tensor
        def _(pe):
            pe.wait_ge(s_par, 16 * 10)
            for i in range(4):
                k, u = divmod(i, 2)
                for jj in range(4):
                    j = 4 * u + jj
                    pe.wait_ge(s_xn, j + 1)
                    ins = pe.transpose(bank[4 + i][:, P * jj:P * jj + P], xn[:, j, P * k:P * k + P], ident[:, :])
                ins.then_inc(s_xnT, 1)
            pe.wait_ge(s_xnTa, 2)
            pe.wait_ge(s_xnTv, 2)

            def channels(w, first):
                for i in range(4):
                    hf, u = i % 2, i // 2
                    for k in range(KC):
                        ins = pe.matmul(bank[i][:, :], w[:, k, P * hf:P * hf + P],
                                        xnT[:, k, 4 * u:4 * u + 4, :].rearrange("p j t -> p (j t)"),
                                        start=(k == 0), stop=(k == KC - 1))
                    ins.then_inc(s_kq, 1)

            pe.wait_ge(s_wkv, 32)
            channels(wk, 0)
            pe.wait_ge(s_wq, 48)
            for j in range(NG):
                for k in range(KC):
                    ins = pe.matmul(bank[4][:, NH * j:NH * j + NH], xnT[:, k, j, :], wlr[:, k, :],
                                    start=(k == 0), stop=(k == KC - 1))
            ins.then_inc(s_eta, 1)
            pe.wait_ge(s_kqc, 4)
            pe.wait_ge(s_wt, 1)
            for j in range(NG):
                bk = bank[5 + j % 3]
                if j >= 3:
                    pe.wait_ge(s_pairT, j - 2)
                for hf in range(KC):
                    pe.transpose(bk[:, P * hf:P * hf + P], xkT[:, hf, j, :], ident[:, :])
                for k in range(KC):
                    pe.matmul(bk[:, 256:512], xnT[:, k, j, :], wt[:, k, :], start=(k == 0), stop=False)
                pe.matmul(bk[:, 256:512], ones_row[:, :], grow[0:1, :], start=False, stop=True).then_inc(s_pair, 1)
            channels(wq, 4)
            pe.wait_ge(s_pairT, NG)
            for f in range(NF):
                for k in range(KC):
                    ins = pe.matmul(bank[7][:, f * NE:(f + 1) * NE], xnT[:, k, f, :], wrt[:, k, :],
                                    start=(k == 0), stop=(k == KC - 1))
            ins.then_inc(s_route, 1)

            def scores(j, q):
                if q == 0:
                    pe.wait_ge(s_xqm, 4 * (j + 1))
                if j or q >= 2:
                    pe.wait_ge(s_mask, 4 * j + q - 1)
                for hf in range(KC):
                    for b in range(B):
                        ins = pe.matmul(bank[2 + q % 2][32 * b:32 * b + 32, P * hf:P * hf + P],
                                        xkT[32 * q:32 * q + 32, hf, j, GT * b:GT * b + GT],
                                        xqm[32 * q:32 * q + 32, j % 2, hf, b, :, :].rearrange("p h t -> p (h t)"),
                                        start=True, stop=True)
                ins.then_inc(s_sc, 1)

            pe.wait_ge(s_kqc, 8)
            pe.wait_ge(s_etaT, 1)
            for q in range(2):
                scores(0, q)
            for i in range(4):
                u, hf = divmod(i, 2)
                if i >= 2:
                    pe.wait_ge(s_tqc, i - 1)
                for b in range(B):
                    ins = pe.transpose(bank[4 + i % 2][:, P * b:P * b + P], xqT[:, hf, b, P * u:P * u + P],
                                       ident[:, :])
                ins.then_inc(s_tq, 1)
            for q in range(2, 4):
                scores(0, q)
            pe.wait_ge(s_wexp, 32)
            pe.wait_ge(s_tqc, 4)

            def gate_up(f, e):
                i = 4 * f + e
                if i >= 2:
                    pe.wait_ge(s_gact, 3 * (i - 1))
                for k in range(KC):
                    ins = pe.matmul(bank[4 + i % 2][:, :], xnT[:, k, f, :],
                                    gup[:, k, 2 * e:2 * e + 2, :].rearrange("p e i -> p (e i)"),
                                    start=(k == 0), stop=(k == KC - 1))
                ins.then_inc(s_gu, 1)

            def hidden(i):
                pe.wait_ge(s_h, i + 1)
                if i >= 1:
                    pe.wait_ge(s_hT, i)
                for r in range(2):
                    ins = pe.transpose(bank[6][:, P * r:P * r + P], hh[:, i % 2, r, :], ident[:, :])
                ins.then_inc(s_hTp, 1)

            def down_proj(i):
                f, e = divmod(i, 4)
                pe.wait_ge(s_hT, i + 1)
                if e == 0 and f:
                    pe.wait_ge(s_g, f)
                for r in range(2):
                    ins = pe.matmul(bank[7][:, 0:HS], hT[:, i % 2, r, :], down[:, 2 * e + r, :],
                                    start=(e == 0 and r == 0), stop=(e == 3 and r == 1))
                ins.then_inc(s_y, 1)

            def group_start(j):
                pe.wait_ge(s_bd, 16 * (j + 2))
                if j == 4:
                    pe.wait_ge(s_zc, 2)
                rows_j = slice(32 * (j % 4), 32 * (j % 4) + 32)
                for hf in range(KC):
                    for b in range(B):
                        ins = pe.matmul(bank[hf][rows_j, :].rearrange("p (h b d) -> p h b d", b=B, d=HD)[:, :, b, :],
                                        xqT[:, hf, b, GT * j:GT * j + GT], bdw[:, j % 2, KC * b + hf, :],
                                        start=(b == 0), stop=False, skip_group_check=True)
                ins.then_inc(s_z0, 1)

            def group_end(j):
                pe.wait_ge(s_sgp, 4 * (j + 1) + 1)
                rows_j = slice(32 * (j % 4), 32 * (j % 4) + 32)
                for h in range(NH):
                    q, c = head_at(h)
                    ins = pe.matmul(bank[h // HH][rows_j, 32 * (h % HH):32 * (h % HH) + 32],
                                    A[:, j % 2, q, GT * c:GT * c + GT],
                                    sgpad[:, j % 2, h, :, :].rearrange("p b d -> p (b d)"),
                                    start=False, stop=False, skip_group_check=True)
                ins.then_inc(s_z, 1)

            def half_end(u):
                for hf in range(KC):
                    ins = pe.matmul(bank[hf][:, :], sel[:, :], biasr[:, u, 512 * hf:512 * hf + 512],
                                    start=False, stop=True, skip_group_check=True)
                ins.then_inc(s_zh, 1)

            for j in range(NG):
                group_start(j)
                for e in range(4):
                    gate_up(j, e)
                    if j + 1 < NG:
                        scores(j + 1, e)
                    hidden(4 * j + e)
                    down_proj(4 * j + e)
                group_end(j)
                if j % 4 == 3:
                    half_end(j // 4)
            pe.wait_ge(s_late, 32)
            pe.wait_ge(s_g, NG)
            for u in range(2):
                for b in range(B):
                    i = 4 * u + b
                    pe.wait_ge(s_yn, i + 1)
                    if i >= 2:
                        pe.wait_ge(s_yT, 2 * (i - 1))
                    for k in range(KC):
                        ins = pe.transpose(bank[2 + i % 2][:, P * k:P * k + P], yn[:, u, b, P * k:P * k + P], ident[:, :])
                    ins.then_inc(s_yTp, 1)
                pe.wait_ge(s_yT, 8 * (u + 1))
                for j in range(4 * u, 4 * u + 4):
                    if j >= 2:
                        pe.wait_ge(s_res1, j - 1)
                    for k in range(KC):
                        ins = pe.matmul(bank[4 + j % 2][:, 0:HS], yT[:, k, j % 4, :], wo[:, k, :],
                                        start=(k == 0), stop=(k == KC - 1))
                    ins.then_inc(s_o, 1)


def kernel(**inputs):
    import numpy as np
    import concourse.bacc as bacc
    from concourse.bass_utils import run_bass_kernel_spmd

    a = {k: np.ascontiguousarray(w) for k, w in inputs.items()}

    def in_major(w):
        return w.T.reshape(KC, P, -1).transpose(1, 0, 2)

    def rep(w):
        return np.broadcast_to(w.reshape(1, -1), (P, w.size))

    def pairs(w):
        return np.broadcast_to(w.reshape(1, NH, -1), (B, NH, w.size // NH)).reshape(P, -1)

    x = a["L0_attn_hidden_states"]
    gu = a["L0_ffn_expert_gate_up"].reshape(NE, KC, P, NI, 2).transpose(2, 1, 0, 4, 3).reshape(P, KC, NE, 2 * NI)
    p = np.arange(P)
    s, t = p[:, None] % GT, np.arange(GT)[None, :]
    arrays = {
        "x_bt": x.reshape(B, NG, GT, HS).transpose(0, 2, 1, 3).reshape(P, NG, HS),
        "wk": in_major(a["L0_attn_k_w"]), "wv": in_major(a["L0_attn_v_w"]),
        "wq": in_major(a["L0_attn_q_w"]), "wo": in_major(a["L0_attn_o_w"]),
        "wlr": in_major(a["L0_attn_ttt_lr_weight"].reshape(NH, HS)),
        "wrt": in_major(a["L0_ffn_router_gate"]),
        "gup": gu,
        "down": a["L0_ffn_expert_down"].transpose(1, 0, 2),
        "pair": np.concatenate([pairs(a["L0_attn_ttt_norm_weight"]), pairs(a["L0_attn_ttt_norm_bias"]),
                                pairs(a["L0_attn_W1"]), pairs(a["L0_attn_b1"]), pairs(a["L0_attn_ttt_lr_bias"])], 1),
        "rows": np.stack([rep(a["L0_attn_ttt_norm_weight"]), rep(a["L0_attn_ttt_norm_bias"])], 1),
        "lti": rep(a["L0_attn_learnable_token_idx"]),
        "post": np.stack([a["L0_attn_post_norm_weight"].reshape(KC, P).T, a["L0_attn_post_norm_bias"].reshape(KC, P).T], 1),
        "ident": np.eye(P), "hmask": (p[:, None] // HD % 4 == np.arange(4)[None, :]),
        "mask_tok": ((s // K == t // K) & (s <= t)) * (-1.0 / HD), "mask_last": (s // K < t // K) * (-1.0 / HD),
        "sel": (np.arange(4)[:, None] == p[None, :] // GT), "iota": rep(np.arange(NE)),
        "inv": rep(1.0 / np.arange(1, K + 1)),
    }
    arrays = {f"in_{k}": np.ascontiguousarray(w, dtype=np.float32) for k, w in arrays.items()}
    nc = bacc.Bacc("TRN2", target_bir_lowering=False, num_devices=1)
    aps = [nc.dram_tensor(k, w.shape, F32, kind="ExternalInput").ap() for k, w in arrays.items()]
    out = nc.dram_tensor("out", (P, NF, HS), F32, kind="ExternalOutput").ap()
    build(nc, *aps, out)
    r = run_bass_kernel_spmd(nc, [arrays], core_ids=[0])
    return r.results[0]["out"].reshape(B, GT, NG, HS).transpose(0, 2, 1, 3).reshape(B, L, HS)
```

```python
import concourse.bass as bass
from concourse import mybir
from contextlib import ExitStack

F32 = mybir.dt.float32
U32 = mybir.dt.uint32
ALU = mybir.AluOpType
ACT = mybir.ActivationFunctionType
AX = mybir.AxisListType

P = 128
B, L, HS = 4, 256, 256
NH, HD, K = 32, 8, 16
NG = 8
GT = L // NG
KC = HS // P
HH = P // HD
C1 = HD + 1
NE, NI = 8, 128
NF = 2 * B
NS = NF * NE // 2
SLOTS = [0, 3, 3, 3, 3, 3, 3, 3]
SMALL_WIDTHS = dict(gam=HD, bet=HD, w0=C1 * HD, lrb=1, gam_row=HS, bet_row=HS, lti=K, inv=K, iota=NE, hmask=4,
                    cmask=4, mask_tok=GT, mask_last=GT, post_w=KC, post_b=KC, ident=P, sel=P)
SMALL, SMALL_N = {}, 0
for name, width in SMALL_WIDTHS.items():
    SMALL[name] = (SMALL_N, width)
    SMALL_N += width
EPS, EPS_IN = 1e-6, 1e-5
FIRST = NS + 2 - NF
BR = P + 1


def build(nc, x_bt_d, x_tok_d, small_d, wkv_d, wq_d, wlr_d, wrt_d, gup_d, down_d, wo_d, out_d):
    wblk_d = nc.dram_tensor("w_blocks", [B * KC * BR, P], F32, kind="Internal")
    grad_d = nc.dram_tensor("grad_rows", [P, HS], F32, kind="Internal")

    with ExitStack() as ctx:
        def sb(name, shape, dt=F32):
            return ctx.enter_context(nc.sbuf_tensor(name, shape, dt))

        def sem(name):
            return ctx.enter_context(nc.semaphore(name))

        bank = [ctx.enter_context(nc.psum_tensor(f"bank{i}", [P, 512], F32)) for i in range(8)]

        x_bt = sb("x_bt", [P, NG, HS])
        small = sb("small", [P, SMALL_N])
        wkv = sb("wkv", [P, 2, KC, HS])
        wq = sb("wq", [P, KC, HS])
        wo = sb("wo", [P, KC, HS])
        wlr = sb("wlr", [P, KC, NH])
        wrt = sb("wrt", [P, KC, NE])
        gup = sb("gup", [P, KC, NE, 2 * NI])
        down = sb("down", [P, NE, HS])
        x_tok = sb("x_tok", [P, NF, HS])
        wk, wv = wkv[:, 0], wkv[:, 1]

        def part(name):
            a, n = SMALL[name]
            return small[:, a:a + n]

        ident, hmask, cmask, mask_tok, mask_last, iota, inv, lti = (
            part(k) for k in ("ident", "hmask", "cmask", "mask_tok", "mask_last", "iota", "inv", "lti"))
        sel = small[0:4, SMALL["sel"][0]:SMALL["sel"][0] + P]
        gam_row, bet_row = part("gam_row"), part("bet_row")
        gam, bet, w0, lrb = part("gam"), part("bet"), part("w0"), part("lrb")
        post_w, post_b = part("post_w"), part("post_b")

        xn = sb("xn", [P, NG, HS])
        xnT = sb("xnT", [P, KC, NG, P])
        xnL = sb("xnL", [P, KC, B, L])
        ones_row = sb("ones_row", [1, P])
        eps_in = sb("eps_in", [P, 1])
        eps = sb("eps", [P, 1])
        stats = sb("stats", [P, NG, 6])
        mv = sb("mv", [P, NG, 2])
        std_in = sb("std_in", [P, NG])
        rstd_in = sb("rstd_in", [P, NG])
        wt = sb("wt", [P, KC, HS])
        wtree = sb("wtree", [P, KC * HS // 2])
        grow = sb("grow", [P, HS])
        growtree = sb("growtree", [P, HS // 2])
        tok = sb("tok", [P, K])
        ntok = sb("ntok", [P, 1])
        mask = sb("mask", [P, GT])
        mask2 = sb("mask2", [P, GT])
        g2 = sb("g2", [P, HD])

        xkT = sb("xkT", [P, KC, NG, P])
        xqT = sb("xqT", [P, KC, B, L])
        xkm = sb("xkm", [P, 2, KC, B, 4, GT])
        KP = sb("KP", [P, 2, C1, GT])
        QP = sb("QP", [P, 2, HD, GT])
        eta = sb("eta", [P, NG * GT])
        sig = sb("sig", [P, NG * GT])

        W = sb("W", [P, 2, C1 * HD])
        wmean = sb("wmean", [P, C1])
        pr1 = sb("pr1", [P, HD * K * C1])
        pr2 = sb("pr2", [P, C1 * HD * K])
        T = sb("T", [P, 5, HD * K])
        S = sb("S", [P, 3, K])
        sxx = sb("sxx", [P, K])
        var = sb("var", [P, K])
        rr = sb("rr", [P, 2, K])
        rs = sb("rs", [P, 2, K])
        a3 = sb("a3", [P, 2, K])
        cf = sb("cf", [P, 4, K])
        hb = sb("hb", [P, 5, HD * K])
        sgb = sb("sgb", [P, HD, GT])
        sgT = sb("sgT", [P, HS])
        sg4 = sb("sg4", [P, 2, B, NH // 4, HD])
        sgpad = sb("sgpad", [P, 2, B, NH // 4, 4, HD])
        dW = sb("dW", [P, C1 * HD])
        A = sb("A", [P, 2, 4, KC * B * GT])
        wblk = sb("wblk", [P, 2, B * KC, P])
        biasr = sb("biasr", [4, 2, B * HS])

        mx = sb("mx", [P, NF, 8])
        mi = sb("mi", [P, NF, 8], U32)
        mif = sb("mif", [P, NF, 2])
        gap = sb("gap", [P, NF])
        s12 = sb("s12", [P, 2, NF])
        oh = sb("oh", [P, 2, NF, NE])
        wexp = sb("wexp", [P, NF, NE])
        gate = sb("gate", [P, 2, 2, NI])
        upw = sb("upw", [P, 2, 2, NI])
        hh = sb("hh", [P, 2, 2, NI])
        hT = sb("hT", [P, 2, 2, P])
        G = sb("G", [P, NF, HS])
        warm = sb("warm", [P, 2 * NG])

        xqb = sb("xqb", [P, 2, B, HS])
        zc = x_bt[:, :, :].rearrange("p (u b) c -> p u (b c)", u=2)
        yn = xn[:, :, :].rearrange("p (u b) c -> p u b c", u=2)
        zsq = wkv[:, :, :, :].rearrange("p w k c -> p w (k c)")
        zg = sb("zg", [P, 2, 512])
        zv = sb("zv", [P, 2, 64])
        zs = sb("zs", [P, 2, 64])
        zr = sb("zr", [P, 2, 64])
        o = zg
        ostat = sb("ostat", [P, B, 6])
        omv = sb("omv", [P, B, 2])
        osd = sb("osd", [P, B])
        ors = sb("ors", [P, B])
        yT = sb("yT", [P, 2, KC, P])

        names = """x_a x_b small wkv wq wlr wrt gup down wo xt
            dve0 pool0 var std xn xnT xnTc kch kchc qch qchc eta etaT sig wt
            pair0 pair0T rows rowsc xqb route gap s12 wx rdve
            zero_w zero_d keys tile tile_done chain vrc rstd sg w w_saved w_loaded b_saved
            sgT sg_out sg_in sgp z0 z zh zc gu gact h hTp hT y g
            zg zv zs post0 ov os yn yTp yT o res fin out"""
        S_ = {n: sem("s_" + n) for n in names.split()}
        ROWS = slice(0, P)

        block = ctx.enter_context(nc.Block())

        def f_bank(f):
            return 2 + f % 2

        hmask8 = hmask.unsqueeze(1).unsqueeze(3).broadcast_to([P, B * NH // 4, 4, HD])

        @block.sync
        def _(sp):
            sp.dma_start(x_bt[:, 0:4, :], x_bt_d[:, 0:4, :]).then_inc(S_["x_a"], 16)
            sp.dma_start(x_bt[:, 4:8, :], x_bt_d[:, 4:8, :]).then_inc(S_["x_b"], 16)
            sp.dma_start(wq[:, :, :], wq_d).then_inc(S_["wq"], 16)
            sp.dma_start(wrt[:, :, :], wrt_d).then_inc(S_["wrt"], 16)
            sp.wait_ge(S_["zero_w"], 1)
            sp.dma_start(bass.AP(wblk_d, 0, [[P, P], [BR * P, B * KC], [1, P]]), wblk[:, 0, :, :]).then_inc(S_["zero_d"], 16)
            sp.dma_start(gup[:, :, :, :], gup_d).then_inc(S_["gup"], 16)
            sp.dma_start(down[:, :, :], down_d).then_inc(S_["down"], 16)
            sp.dma_start(wo[:, :, :], wo_d).then_inc(S_["wo"], 16)
            sp.wait_ge(S_["zero_d"], 16)

            def save_w(j):
                sp.wait_ge(S_["w"], 2 * j + 1)
                if j:
                    sp.wait_ge(S_["w_loaded"], 16 * j)
                sp.dma_start(bass.AP(wblk_d, 0, [[HD * P + HD, P], [P, HD], [1, HD]]),
                             W[:, 0, 0:HD * HD].rearrange("p (c d) -> p c d", d=HD)).then_inc(S_["w_saved"], 16)

            def load_w(j):
                sp.wait_ge(S_["w_saved"], 16 * (j + 1))
                if j >= 2:
                    sp.wait_ge(S_["z0"], j - 1)
                sp.dma_start(wblk[:, j % 2, :, :],
                             bass.AP(wblk_d, 0, [[P, P], [BR * P, B * KC], [1, P]])).then_inc(S_["w_loaded"], 16)

            def save_b(j):
                if j:
                    sp.wait_ge(S_["b_saved"], 16 * j)
                sp.dma_start(biasr[j % 4:j % 4 + 1, j // 4, :].rearrange("p (q d) -> p q d", d=HD),
                             W[:, 0, HD * HD:]).then_inc(S_["b_saved"], 16)

            def save_grads(j):
                sp.wait_ge(S_["sgT"], j + 1)
                if j:
                    sp.wait_ge(S_["sg_in"], 64 * j)
                sp.dma_start(bass.AP(grad_d, 0, [[HS, P], [1, HS]]), sgT[:, :]).then_inc(S_["sg_out"], 16)

            def load_grads(j):
                sp.wait_ge(S_["sg_out"], 16 * (j + 1))
                if j >= 2:
                    sp.wait_ge(S_["sgp"], j - 1)
                for h in range(4):
                    sp.dma_start(sg4[GT * h:GT * h + GT, j % 2, :, :, :].rearrange("p b q d -> p b (q d)"),
                                 bass.AP(grad_d, NH // 4 * HD * h, [[HS, GT], [GT * HS, B], [1, NH // 4 * HD]])
                                 ).then_inc(S_["sg_in"], 16)

            save_w(0)
            load_w(0)
            save_b(0)
            for j in range(NG):
                if j + 1 < NG:
                    save_w(j + 1)
                save_grads(j)
                if j + 1 < NG:
                    load_w(j + 1)
                load_grads(j)
                if j + 1 < NG:
                    save_b(j + 1)
                if j == 3:
                    sp.dma_start(x_tok[:, :, :], x_tok_d).then_inc(S_["xt"], 16)
            for f in range(0, NF, 2):
                sp.wait_ge(S_["fin"], f + 2)
                sp.dma_start(out_d[:, f:f + 2, :], G[:, f:f + 2, :]).then_inc(S_["out"], 16)
            sp.wait_ge(S_["out"], 16 * NF // 2)

        @block.gpsimd
        def _(pool):
            pool.memset(ones_row[:, :], 1.0).then_inc(S_["pool0"], 1)
            pool.memset(KP[:, :, HD, :], 1.0).then_inc(S_["pool0"], 1)
            n = [2]

            def link(ins):
                n[0] += 1
                ins.then_inc(S_["pool0"], 1)
                pool.wait_ge(S_["pool0"], n[0])

            def centre(full, tree, m):
                v = full.rearrange("p (m d) -> p m d", d=HD)
                t4 = tree.rearrange("p (m d) -> p m d", d=4)
                link(pool.tensor_tensor(t4, v[:, :, 0:4], v[:, :, 4:8], ALU.add))
                link(pool.tensor_tensor(t4[:, :, 0:2], t4[:, :, 0:2], t4[:, :, 2:4], ALU.add))
                link(pool.tensor_tensor(t4[:, :, 0:1], t4[:, :, 0:1], t4[:, :, 1:2], ALU.add))
                link(pool.tensor_scalar(t4[:, :, 0:1], t4[:, :, 0:1], -1.0 / HD, 0.0, ALU.mult, ALU.add))
                return pool.tensor_tensor(v, v, t4[:, :, 0:1].broadcast_to([P, m, HD]), ALU.add)

            pool.wait_ge(S_["small"], 16)
            link(pool.tensor_tensor(grow[:, :], gam_row, bet_row, ALU.mult))
            link(centre(grow[:, :], growtree[:, :], NH))
            pool.wait_ge(S_["wkv"], 16)
            link(pool.tensor_tensor(wt[:, :, :], wk, wv, ALU.subtract))
            link(pool.tensor_tensor(wt[:, :, :], wt[:, :, :], gam_row.unsqueeze(1).broadcast_to([P, KC, HS]), ALU.mult))
            centre(wt[:, :, :].rearrange("p a b -> p (a b)"), wtree[:, :], KC * NH).then_inc(S_["wt"], 1)
            pool.memset(wblk[:, 0, :, :], 0.0).then_inc(S_["zero_w"], 1)

            def masked_keys(j):
                pool.wait_ge(S_["kchc"], 2 + 2 * (j // 4))
                if j >= 2:
                    pool.wait_ge(S_["tile"], 5 * (j - 1))
                for h in range(4):
                    pool.tensor_scalar(xkm[:, j % 2, :, :, h, :],
                                       xkT[:, :, j, :].rearrange("p k (b t) -> p k b t", b=B),
                                       cmask[:, h:h + 1], 0.0, ALU.mult, ALU.add).then_inc(S_["keys"], 1)

            def hidden_product(i):
                pool.wait_ge(S_["gact"], 3 * (i + 1))
                if i >= 2:
                    pool.wait_ge(S_["hTp"], i - 1)
                pool.tensor_tensor(hh[:, i % 2, :, :], gate[:, i % 2, :, :], upw[:, i % 2, :, :],
                                   ALU.mult).then_inc(S_["h"], 1)

            def half_scale(u):
                for k in range(2):
                    pool.wait_ge(S_["zc"], 4 * u + 2 * k + 2)
                    if u:
                        pool.wait_ge(S_["yn"], 2 * (k + 1))
                    pool.tensor_tensor(zg[:, k, :].rearrange("p (b c) -> p b c", c=HS),
                                       zc[:, u, 512 * k:512 * k + 512].rearrange("p (b c) -> p b c", c=HS),
                                       gam_row.unsqueeze(1).broadcast_to([P, 2, HS]), ALU.mult).then_inc(S_["zg"], 1)

            def pad_grads(j):
                pool.wait_ge(S_["sg_in"], 64 * (j + 1))
                if j >= 2:
                    pool.wait_ge(S_["z"], j - 1)
                pool.tensor_tensor(sgpad[:, j % 2, :, :, :, :].rearrange("p b q h d -> p (b q) h d"),
                                   sg4[:, j % 2, :, :, :].rearrange("p b q d -> p (b q) d").unsqueeze(2)
                                   .broadcast_to([P, B * NH // 4, 4, HD]),
                                   hmask8, ALU.mult).then_inc(S_["sgp"], 1)

            def residual(f):
                pool.wait_ge(S_["res"], f + 1)
                pool.tensor_tensor(G[:, f, :], G[:, f, :], x_tok[:, f, :], ALU.add).then_inc(S_["fin"], 1)

            slot = 0
            masked_keys(0)
            for j in range(NG):
                if j + 1 < NG:
                    masked_keys(j + 1)
                if j == 1:
                    pool.wait_ge(S_["rowsc"], 4)
                    for u in range(2):
                        pool.tensor_tensor(xqb[:, u, :, :], xqb[:, u, :, :],
                                           bet_row.unsqueeze(1).broadcast_to([P, B, HS]), ALU.add).then_inc(S_["xqb"], 1)
                if j == 6:
                    half_scale(0)
                for i in range(slot, slot + SLOTS[j] // 2):
                    hidden_product(i)
                if j:
                    pad_grads(j - 1)
                for i in range(slot + SLOTS[j] // 2, slot + SLOTS[j]):
                    hidden_product(i)
                slot += SLOTS[j]
            for i in range(slot, NS):
                hidden_product(i)
                if i == slot:
                    pad_grads(NG - 1)
                if i == slot + 4:
                    half_scale(1)
            pool.wait_ge(S_["xt"], 16)
            for f in range(NF):
                residual(f)

        @block.scalar
        def _(act):
            act.dma_start(small[:, :], small_d).then_inc(S_["small"], 16)
            act.dma_start(wkv[:, :, :, :], wkv_d).then_inc(S_["wkv"], 16)
            act.dma_start(wlr[:, :, :], wlr_d).then_inc(S_["wlr"], 16)

            def input_std(u):
                act.wait_ge(S_["var"], u + 1)
                if u == 0:
                    act.wait_ge(S_["dve0"], 2)
                act.activation(std_in[:, 4 * u:4 * u + 4], mv[:, 4 * u:4 * u + 4, 1], ACT.Sqrt,
                               bias=eps_in[:, 0:1]).then_inc(S_["std"], 1)

            def xn_out(u):
                for k in range(KC):
                    i = 2 * u + k
                    act.wait_ge(S_["xnT"], i + 1)
                    act.copy(xnT[:, k, 4 * u:4 * u + 4, :].rearrange("p j t -> p (j t)"), bank[4 + i][:, :]).then_inc(S_["xnTc"], 1)

            def channels_out(name, u):
                for hf in range(KC):
                    act.wait_ge(S_[name], 2 * u + hf + 1)
                    if name == "kch":
                        act.copy(xkT[:, hf, 4 * u:4 * u + 4, :].rearrange("p j t -> p (j t)"),
                                 bank[hf][:, :]).then_inc(S_["kchc"], 1)
                    else:
                        act.copy(xqT[:, hf, :, P * u:P * u + P].rearrange("p b (j t) -> p j b t", t=GT),
                                 bank[hf][:, :].rearrange("p (j b t) -> p j b t", j=4, b=B)).then_inc(S_["qchc"], 1)

            def rates(u):
                act.wait_ge(S_["etaT"], u + 1)
                act.activation(sig[:, P * u:P * u + P], eta[:, P * u:P * u + P], ACT.Sigmoid,
                               bias=lrb).then_inc(S_["sig"], 1)

            def query_rows(u):
                for i in range(2 * u, 2 * u + 2):
                    act.wait_ge(S_["rows"], i + 1)
                    act.copy(xqb[:, u, :, P * (i % 2):P * (i % 2) + P],
                             bank[4 + i % 2][:, :].rearrange("p (b c) -> p b c", b=B)).then_inc(S_["rowsc"], 1)

            def step_std(n):
                act.wait_ge(S_["vrc"], n + 1)
                act.activation(rr[:, 0, :], rr[:, 1, :], ACT.Sqrt).then_inc(S_["rstd"], 1)

            def expert_slot(i):
                f, e = divmod(i, 4)
                if i < NS:
                    bk = bank[4 + i % 2][:, :].rearrange("p (e g i) -> p e g i", e=2, g=2)
                    act.wait_ge(S_["gu"], i + 1)
                    if i >= 2:
                        act.wait_ge(S_["h"], i - 1)
                    act.activation(gate[:, i % 2, :, :], bk[:, :, 0, :], ACT.Silu).then_inc(S_["gact"], 1)
                    for r in range(2):
                        act.activation(upw[:, i % 2, r, :], bk[:, r, 1, :], ACT.Copy,
                                       scale=wexp[:, f, 2 * e + r:2 * e + r + 1]).then_inc(S_["gact"], 1)
                if 1 <= i <= NS:
                    act.wait_ge(S_["hTp"], i)
                    if i >= 3:
                        act.wait_ge(S_["y"], i - 2)
                    act.copy(hT[:, (i - 1) % 2, :, :].rearrange("p e t -> p (e t)"), bank[6][:, 0:2 * P]).then_inc(S_["hT"], 1)
                if i >= 5 and e == 1:
                    act.wait_ge(S_["y"], i - 1)
                    act.activation(G[:, f - 1, :], bank[7][:, 0:HS], ACT.Silu).then_inc(S_["g"], 1)

            def preload_sqrt(n):
                act.activation(warm[:, n:n + 1], eps[:, :], ACT.Sqrt)

            def half_out(u):
                for k in range(2):
                    act.wait_ge(S_["zh"], 2 * u + k + 1)
                    if u:
                        act.wait_ge(S_["zv"], k + 1)
                    act.activation(zsq[:, k, :], bank[k][:, :], ACT.Square).then_inc(S_["zc"], 1)
                    act.copy(zc[:, u, 512 * k:512 * k + 512], bank[k][:, :]).then_inc(S_["zc"], 1)

            def norm_z(u):
                for k in range(2):
                    act.wait_ge(S_["zv"], 2 * u + k + 1)
                    act.activation(zs[:, k, :], zv[:, k, :], ACT.Sqrt, bias=eps[:, 0:1], scale=1.0 / HD).then_inc(S_["zs"], 1)

            def norm_o(u):
                for k in range(2):
                    act.wait_ge(S_["ov"], 2 * u + k + 1)
                    act.activation(osd[:, 2 * k:2 * k + 2], omv[:, 2 * k:2 * k + 2, 1], ACT.Sqrt,
                                   bias=eps[:, 0:1]).then_inc(S_["os"], 1)

            def post_rows(f):
                act.wait_ge(S_["yTp"], f + 1)
                if f >= 2:
                    act.wait_ge(S_["o"], f - 1)
                for k in range(KC):
                    act.activation(yT[:, f % 2, k, :], bank[f_bank(f)][:, P * k:P * k + P], ACT.Identity,
                                   scale=post_w[:, k:k + 1], bias=post_b[:, k:k + 1]).then_inc(S_["yT"], 1)

            input_std(0)
            input_std(1)
            xn_out(0)
            channels_out("kch", 0)
            rates(0)
            xn_out(1)
            channels_out("qch", 0)
            preload_sqrt(0)
            step_std(0)
            for k in range(KC):
                for u in range(2):
                    act.copy(xnL[:, k, :, P * u:P * u + P].rearrange("p b (j t) -> p j b t", t=GT),
                             xnT[:, k, 4 * u:4 * u + 4, :].rearrange("p j (b t) -> p j b t", b=B)).then_inc(S_["xnTc"], 1)
            channels_out("kch", 1)
            query_rows(0)
            step_std(1)
            channels_out("qch", 1)
            query_rows(1)
            rates(1)
            act.wait_ge(S_["gap"], 1)
            act.activation(s12[:, 0, :], gap[:, :], ACT.Sigmoid).then_inc(S_["s12"], 1)
            act.activation(s12[:, 1, :], gap[:, :], ACT.Sigmoid, scale=-1.0).then_inc(S_["s12"], 1)
            preload_sqrt(1)
            slot = 0
            for j in range(1, NG):
                for m in range(2):
                    step_std(2 * j + m)
                    if j == 1 and m == 0:
                        act.wait_ge(S_["wx"], 1)
                    if j == 5 and m == 0:
                        half_out(0)
                    for i in range(slot + m * (SLOTS[j] // 2), slot + (SLOTS[j] // 2 if m == 0 else SLOTS[j])):
                        expert_slot(i)
                    if j + m < NG:
                        preload_sqrt(2 * j + m)
                slot += SLOTS[j]
            after = {1: [lambda: norm_z(0)], 2: [lambda: norm_o(0)], 3: [lambda: half_out(1)],
                     6: [lambda: norm_z(1)], 7: [lambda: norm_o(1)]}
            for i in range(slot, NS + 2):
                expert_slot(i)
                for step in after.get(i - slot + 1, []):
                    step()
                if i >= FIRST:
                    post_rows(i - FIRST)

        @block.vector
        def _(v):
            n0 = [0]

            def link(ins, semaphore=S_["dve0"], count=n0):
                count[0] += 1
                ins.then_inc(semaphore, 1)
                v.wait_ge(semaphore, count[0])

            link(v.memset(eps_in[:, :], EPS_IN))
            link(v.memset(eps[:, :], EPS))

            def input_stats(u):
                v.wait_ge(S_["x_b" if u else "x_a"], 16)
                for j in range(4 * u, 4 * u + 4):
                    ins = v.bn_stats(stats[:, j, :], x_bt[:, j, :])
                link(ins)
                for j in range(4 * u, 4 * u + 4):
                    ins = v.bn_aggr(mv[:, j, :], stats[:, j, :])
                ins.then_inc(S_["var"], 1)

            def input_norm(u):
                v.wait_ge(S_["std"], u + 1)
                link(v.reciprocal(rstd_in[:, 4 * u:4 * u + 4], std_in[:, 4 * u:4 * u + 4]))
                for j in range(4 * u, 4 * u + 4):
                    v.tensor_scalar(xn[:, j, :], x_bt[:, j, :], mv[:, j, 0:1], rstd_in[:, j:j + 1],
                                    ALU.subtract, ALU.mult).then_inc(S_["xn"], 1)

            input_stats(0)
            input_stats(1)
            input_norm(0)
            v.wait_ge(S_["small"], 16)
            link(v.tensor_tensor(g2[:, :], gam, gam, ALU.mult))
            link(v.tensor_reduce(wmean[:, :], w0.rearrange("p (c d) -> p c d", d=HD), AX.X, ALU.add))
            link(v.tensor_scalar(wmean[:, :], wmean[:, :], -1.0 / HD, None, ALU.mult))
            v.tensor_tensor(W[:, 0, :].rearrange("p (c d) -> p c d", d=HD), w0.rearrange("p (c d) -> p c d", d=HD),
                            wmean[:, :].unsqueeze(2).broadcast_to([P, C1, HD]), ALU.add).then_inc(S_["w"], 1)
            link(v.tensor_tensor(tok[:, :], inv, lti, ALU.add))
            link(v.tensor_scalar(tok[:, :], tok[:, :], 0.0, None, ALU.max))
            input_norm(1)
            link(v.tensor_scalar(ntok[:, :], tok[:, K - 1:K], -1.0 / HD, None, ALU.mult))
            link(v.tensor_tensor(mask[:, :].rearrange("p (m t) -> p m t", t=K),
                                 mask_tok.rearrange("p (m t) -> p m t", t=K),
                                 tok[:, :].unsqueeze(1).broadcast_to([P, 2, K]), ALU.mult))
            link(v.tensor_scalar(mask2[:, :], mask_last, tok[:, K - 1:K], None, ALU.mult))
            link(v.tensor_tensor(mask[:, :], mask[:, :], mask2[:, :], ALU.add))

            def rates_to_pairs(u):
                v.wait_ge(S_["eta"], u + 1)
                v.transpose(eta[:, P * u:P * u + P], bank[7][:, P * u:P * u + P]).then_inc(S_["etaT"], 1)

            def group_to_pairs(ring, bk):
                v.transpose(KP[:, ring, 0:HD, :],
                            bk[:, 0:256].rearrange("p (h c) -> p c h", c=HD))
                return v.transpose(QP[:, ring, :, :],
                                   bk[:, 256:512].rearrange("p (h c) -> p c h", c=HD))

            r0 = [0]

            def route_gap():
                v.wait_ge(S_["route"], 1)
                logits = bank[7][:, 256:256 + NF * NE].rearrange("p (f e) -> p f e", e=NE)
                for f in range(NF):
                    ins = v.max(mx[:, f, :], logits[:, f, :])
                link(ins, S_["rdve"], r0)
                v.tensor_tensor(gap[:, :], mx[:, :, 0], mx[:, :, 1], ALU.subtract).then_inc(S_["gap"], 1)
                for f in range(NF):
                    ins = v.max_index(mi[:, f, :], mx[:, f, :], logits[:, f, :])
                link(ins, S_["rdve"], r0)
                link(v.tensor_copy(mif[:, :, :], mi[:, :, 0:2]), S_["rdve"], r0)

            def route_weights():
                for k in range(2):
                    link(v.tensor_tensor(oh[:, k, :, :], iota.unsqueeze(1).broadcast_to([P, NF, NE]),
                                         mif[:, :, k:k + 1].broadcast_to([P, NF, NE]), ALU.is_equal), S_["rdve"], r0)
                v.wait_ge(S_["s12"], 2)
                for k in range(2):
                    link(v.tensor_tensor(oh[:, k, :, :], oh[:, k, :, :],
                                         s12[:, k, :].unsqueeze(2).broadcast_to([P, NF, NE]), ALU.mult), S_["rdve"], r0)
                v.tensor_tensor(wexp[:, :, :], oh[:, 0, :, :], oh[:, 1, :, :], ALU.add).then_inc(S_["wx"], 1)

            mask_bc = mask[:, :].unsqueeze(1).broadcast_to([P, KC * B, GT])

            def take_tile(j, ring, i, last):
                bk = bank[2 + (5 * ring + i) % 2]
                v.wait_ge(S_["tile"], j * 5 + i + (0 if last else 1))
                if i == 0:
                    ins = group_to_pairs(1 - ring, bk)
                else:
                    ins = v.scalar_tensor_tensor(
                        out=A[:, ring, i - 1, :].rearrange("p (h t) -> p h t", t=GT),
                        in0=bk[:, 0:256].rearrange("p (h t) -> p h t", t=GT), scalar=1.0, in1=mask_bc,
                        op0=ALU.add, op1=ALU.mult)
                ins.then_inc(S_["tile_done"], 1)

            OPS = 16

            def minibatch(j, ring, m, fill, last=False):
                n = j * 2 + m
                Wn = W[:, m, :]
                kp, qn = KP[:, ring, :, K * m:K * m + K], QP[:, ring, :, K * m:K * m + K]
                sg_n = sig[:, bass.ds(j * GT + K * m, K)]
                chain = S_["chain"]
                done = lambda k: v.wait_ge(chain, n * OPS + k)
                dt = lambda a: a.rearrange("p (d t) -> p d t", d=HD)
                b3 = lambda a: a.unsqueeze(1).broadcast_to([P, HD, K])
                x, u, pq, ux, xx = (dt(T[:, i, :]) for i in range(5))

                v.wait_ge(S_["w"], n + 1)
                if m == 0 and (not isinstance(j, int) or j):
                    v.wait_ge(S_["tile_done"], 5 * (j - 1) + 1)
                v.tensor_tensor(pr1[:, :].rearrange("p (d t c) -> p d t c", d=HD, t=K),
                                kp.rearrange("p c t -> p t c").unsqueeze(1).broadcast_to([P, HD, K, C1]),
                                Wn.rearrange("p (c d) -> p d c", d=HD).unsqueeze(2).broadcast_to([P, HD, K, C1]),
                                ALU.mult).then_inc(chain, 1)
                fill(0)
                done(1)
                v.tensor_reduce(T[:, 0, :], pr1[:, :].rearrange("p (a c) -> p a c", c=C1), AX.X,
                                ALU.add).then_inc(chain, 1)
                done(2)
                v.tensor_tensor(xx, x, x, ALU.mult).then_inc(chain, 1)
                v.tensor_tensor(u, x, g2[:, :].unsqueeze(2).broadcast_to([P, HD, K]), ALU.mult).then_inc(chain, 1)
                done(3)
                v.tensor_reduce(sxx[:, :], xx.rearrange("p d t -> p t d"), AX.X, ALU.add).then_inc(chain, 1)
                v.tensor_tensor(pq, x, qn, ALU.mult).then_inc(chain, 1)
                done(5)
                v.tensor_scalar(var[:, :], sxx[:, :], 1.0 / HD, EPS, ALU.mult, ALU.add).then_inc(chain, 1)
                v.tensor_tensor(ux, x, u, ALU.mult).then_inc(chain, 1)
                done(7)
                v.reciprocal(rr[:, 1, :], var[:, :]).then_inc(S_["vrc"], 1)
                done(8)
                v.tensor_reduce(S[:, :, :], T[:, 1:4, :].rearrange("p k (d t) -> p k t d", d=HD), AX.X,
                                ALU.add).then_inc(chain, 1)
                fill(1)
                v.wait_ge(S_["rstd"], n + 1)
                v.tensor_tensor(cf[:, 3:0:-2, :], rr[:, :, :], sg_n.unsqueeze(1).broadcast_to([P, 2, K]),
                                ALU.mult).then_inc(chain, 1)
                done(9)
                v.tensor_tensor(rs[:, :, :], rr[:, :, :], S[:, 1:3, :], ALU.mult).then_inc(chain, 1)
                done(10)
                v.tensor_tensor(dt(hb[:, 2, :]), qn, b3(cf[:, 3, :]), ALU.mult).then_inc(chain, 1)
                done(11)
                v.tensor_tensor(S[:, 1, :], rs[:, 0, :], rs[:, 1, :], ALU.add).then_inc(chain, 1)
                done(13)
                v.scalar_tensor_tensor(out=cf[:, 2::-2, :], in0=S[:, 0:2, :], scalar=-1.0 / HD,
                                       in1=cf[:, 1:2, :].broadcast_to([P, 2, K]),
                                       op0=ALU.mult, op1=ALU.mult).then_inc(chain, 1)
                done(14)
                v.tensor_tensor(hb[:, 0:2, :].rearrange("p k (d t) -> p k d t", d=HD),
                                T[:, 0:2, :].rearrange("p k (d t) -> p k d t", d=HD),
                                cf[:, 0:2, :].unsqueeze(2).broadcast_to([P, 2, HD, K]), ALU.mult).then_inc(chain, 1)
                v.tensor_tensor(dt(hb[:, 3, :]), dt(hb[:, 2, :]), b3(cf[:, 2, :]), ALU.add).then_inc(chain, 1)
                done(15)
                v.tensor_tensor(dt(hb[:, 4, :]), dt(hb[:, 0, :]), dt(hb[:, 1, :]), ALU.add).then_inc(S_["sg"], 1)
                v.wait_ge(S_["sg"], 4 * n + 1)
                sg = sgb[:, :, K * m:K * m + K]
                v.tensor_tensor(sg, dt(hb[:, 4, :]), dt(hb[:, 3, :]), ALU.add).then_inc(S_["sg"], 1)
                if last:
                    v.wait_ge(S_["sg"], 4 * n + 2)
                    return
                v.wait_ge(S_["sg"], 4 * n + 2)
                v.tensor_tensor(pr2[:, :].rearrange("p (c d t) -> p c d t", c=C1, d=HD),
                                kp.unsqueeze(2).broadcast_to([P, C1, HD, K]),
                                sg.unsqueeze(1).broadcast_to([P, C1, HD, K]), ALU.mult).then_inc(S_["sg"], 1)
                fill(2)
                v.wait_ge(S_["sg"], 4 * n + 3)
                v.tensor_reduce(dW[:, :], pr2[:, :].rearrange("p (a t) -> p a t", t=K), AX.X,
                                ALU.add).then_inc(S_["sg"], 1)
                if m == 1:
                    v.wait_ge(S_["w_saved"], 16 * (j + 1))
                    v.wait_ge(S_["b_saved"], 16 * (j + 1))
                v.wait_ge(S_["sg"], 4 * n + 4)
                v.scalar_tensor_tensor(out=W[:, 1 - m, :], in0=dW[:, :], scalar=ntok[:, 0:1], in1=Wn,
                                       op0=ALU.mult, op1=ALU.add).then_inc(S_["w"], 1)

            def group(j, ring, between=None, last=False):
                plan = {(0, 0): 0, (0, 1): 1, (0, 2): 2, (1, 1): 3, (1, 2): 4}

                def filler(m):
                    def fill(i):
                        if (m, i) in plan and not (last and plan[m, i] == 0):
                            take_tile(j, ring, plan[m, i], last)
                    return fill

                minibatch(j, ring, 0, filler(0))
                if between:
                    between()
                minibatch(j, ring, 1, filler(1), last)
                if last:
                    take_tile(j, ring, 4, last)
                if not isinstance(j, int) or j:
                    v.wait_ge(S_["sg_out"], 16 * j)
                v.transpose(sgT[:, :].rearrange("p (x y d) -> p d y x", x=4, d=HD),
                            sgb[:, :, :].rearrange("p d t -> p (d t)")).then_inc(S_["sgT"], 1)

            def half_post(u):
                p0 = post_count
                for k in range(2):
                    v.wait_ge(S_["zc"], 4 * u + 2 * k + 1)
                    v.tensor_reduce(zv[:, k, :], zsq[:, k, :].rearrange("p (a d) -> p a d", d=HD), AX.X,
                                    ALU.add).then_inc(S_["zv"], 1)
                for k in range(2):
                    v.wait_ge(S_["zs"], 2 * u + k + 1)
                    link(v.reciprocal(zr[:, k, :], zs[:, k, :]), S_["post0"], p0)
                    v.wait_ge(S_["zg"], 2 * u + k + 1)
                    link(v.tensor_tensor(o[:, k, :].rearrange("p (a d) -> p a d", d=HD),
                                         zg[:, k, :].rearrange("p (a d) -> p a d", d=HD),
                                         zr[:, k, :].unsqueeze(2).broadcast_to([P, 64, HD]), ALU.mult), S_["post0"], p0)
                    v.wait_ge(S_["xqb"], 2)
                    link(v.tensor_tensor(o[:, k, :], o[:, k, :],
                                         xqb[:, u, 2 * k:2 * k + 2, :].rearrange("p b c -> p (b c)"), ALU.add), S_["post0"], p0)
                    for b in range(2):
                        ins = v.bn_stats(ostat[:, 2 * k + b, :], o[:, k, HS * b:HS * b + HS])
                    link(ins, S_["post0"], p0)
                    for b in range(2):
                        ins = v.bn_aggr(omv[:, 2 * k + b, :], ostat[:, 2 * k + b, :])
                    ins.then_inc(S_["ov"], 1)
                for k in range(2):
                    v.wait_ge(S_["os"], 2 * u + k + 1)
                    link(v.reciprocal(ors[:, 2 * k:2 * k + 2], osd[:, 2 * k:2 * k + 2]), S_["post0"], p0)
                    for b in range(2):
                        i = 2 * k + b
                        v.tensor_scalar(yn[:, u, i, :], o[:, k, HS * b:HS * b + HS], omv[:, i, 0:1], ors[:, i:i + 1],
                                        ALU.subtract, ALU.mult).then_inc(S_["yn"], 1)

            def gate_rows():
                for f in range(NF):
                    v.wait_ge(S_["o"], f + 1)
                    v.wait_ge(S_["g"], f + 1)
                    v.tensor_tensor(G[:, f, :], bank[f_bank(f)][:, 256:512], G[:, f, :], ALU.mult).then_inc(S_["res"], 1)

            post_count = [0]
            rates_to_pairs(0)
            v.wait_ge(S_["pair0"], 1)
            group_to_pairs(0, bank[6]).then_inc(S_["pair0T"], 1)
            v.wait_ge(S_["sig"], 1)
            v.wait_ge(S_["pool0"], 2)
            v.wait_ge(S_["pair0T"], 1)
            group(0, 0, lambda: rates_to_pairs(1))
            route_gap()
            group(1, 1, route_weights)
            v.wait_ge(S_["sig"], 2)
            with v.Fori(0, 4, 2) as i:
                group(i + 2, 0)
                group(i + 3, 1)
            group(6, 0)
            group(7, 1, last=True)
            half_post(0)
            half_post(1)
            gate_rows()

        @block.tensor
        def _(pe):
            pe.wait_ge(S_["small"], 16)

            def xn_channels(u):
                for k in range(KC):
                    for jj in range(4):
                        j = 4 * u + jj
                        pe.wait_ge(S_["xn"], j + 1)
                        ins = pe.transpose(bank[4 + 2 * u + k][:, P * jj:P * jj + P], xn[:, j, P * k:P * k + P], ident)
                    ins.then_inc(S_["xnT"], 1)

            def channels(w, base, u, name):
                for hf in range(KC):
                    for k in range(KC):
                        ins = pe.matmul(bank[base + hf][:, :], w[:, k, P * hf:P * hf + P],
                                        xnT[:, k, 4 * u:4 * u + 4, :].rearrange("p j t -> p (j t)"),
                                        start=(k == 0), stop=(k == KC - 1))
                    ins.then_inc(S_[name], 1)

            def rates(u):
                for j in range(4 * u, 4 * u + 4):
                    for k in range(KC):
                        ins = pe.matmul(bank[7][:, NH * j:NH * j + NH], xnT[:, k, j, :], wlr[:, k, :],
                                        start=(k == 0), stop=(k == KC - 1))
                ins.then_inc(S_["eta"], 1)

            def pair_rows(j, bk):
                for hf in range(KC):
                    pe.transpose(bk[:, P * hf:P * hf + P], xkT[:, hf, j, :], ident)
                for k in range(KC):
                    pe.matmul(bk[:, 256:512], xnT[:, k, j, :], wt[:, k, :], start=(k == 0), stop=False)
                return pe.matmul(bk[:, 256:512], ones_row[:, :], grow[0:1, :], start=False, stop=True)

            def tile(j, i):
                c = 5 * j + i
                bk = bank[2 + c % 2]
                if c >= 2:
                    pe.wait_ge(S_["tile_done"], c - 1 - (1 if c - 2 >= 5 * (NG - 1) else 0))
                if i == 0:
                    ins = pair_rows(j + 1, bk)
                else:
                    q = i - 1
                    pe.wait_ge(S_["keys"], 4 * (j + 1))
                    for hf in range(KC):
                        for b in range(B):
                            c0 = GT * (B * hf + b)
                            ins = pe.matmul(bk[:, c0:c0 + GT],
                                            xkm[32 * q:32 * q + 32, j % 2, hf, b, :, :].rearrange("p h t -> p (h t)"),
                                            xqT[32 * q:32 * q + 32, hf, b, GT * j:GT * j + GT], start=True, stop=True)
                ins.then_inc(S_["tile"], 1)

            def query_rows(u):
                pe.wait_ge(S_["qchc"], 2 * (u + 1))
                if u:
                    pe.wait_ge(S_["rowsc"], 2)
                for hf in range(KC):
                    for b in range(B):
                        ins = pe.transpose(bank[4 + hf][:, P * b:P * b + P], xqT[:, hf, b, P * u:P * u + P], ident)
                    ins.then_inc(S_["rows"], 1)

            def expert_slot(i):
                if i < NS:
                    f, e = divmod(i, 4)
                    u, b = divmod(f, B)
                    if i >= 2:
                        pe.wait_ge(S_["gact"], 3 * (i - 1))
                    else:
                        pe.wait_ge(S_["rowsc"], 4)
                        pe.wait_ge(S_["gup"], 16)
                    for k in range(KC):
                        ins = pe.matmul(bank[4 + i % 2][:, :], xnL[:, k, b, P * u:P * u + P],
                                        gup[:, k, 2 * e:2 * e + 2, :].rearrange("p e i -> p (e i)"),
                                        start=(k == 0), stop=(k == KC - 1))
                    ins.then_inc(S_["gu"], 1)
                if 1 <= i <= NS:
                    pe.wait_ge(S_["h"], i)
                    if i >= 2:
                        pe.wait_ge(S_["hT"], i - 1)
                    for r in range(2):
                        ins = pe.transpose(bank[6][:, P * r:P * r + P], hh[:, (i - 1) % 2, r, :], ident)
                    ins.then_inc(S_["hTp"], 1)
                if i >= 2:
                    f, e = divmod(i - 2, 4)
                    pe.wait_ge(S_["hT"], i - 1)
                    if i == 2:
                        pe.wait_ge(S_["down"], 16)
                    if e == 0 and f:
                        pe.wait_ge(S_["g"], f)
                    for r in range(2):
                        ins = pe.matmul(bank[7][:, 0:HS], hT[:, i % 2, r, :], down[:, 2 * e + r, :],
                                        start=(e == 0 and r == 0), stop=(e == 3 and r == 1))
                    ins.then_inc(S_["y"], 1)

            def group_start(j):
                pe.wait_ge(S_["w_loaded"], 16 * (j + 1))
                if j == 0:
                    pe.wait_ge(S_["qchc"], 4)
                if j == 4:
                    pe.wait_ge(S_["zc"], 4)
                rows_j = slice(32 * (j % 4), 32 * (j % 4) + 32)
                for b in range(B):
                    for hf in range(KC):
                        c0 = HS * (b % 2) + P * hf
                        ins = pe.matmul(bank[b // 2][rows_j, c0:c0 + P], xqT[:, hf, b, GT * j:GT * j + GT],
                                        wblk[:, j % 2, KC * b + hf, :],
                                        start=(b % 2 == 0 and hf == 0), stop=False, skip_group_check=True)
                ins.then_inc(S_["z0"], 1)

            def group_end(j):
                pe.wait_ge(S_["sgp"], j + 1)
                pe.wait_ge(S_["tile_done"], 5 * (j + 1) - (1 if j == NG - 1 else 0))
                rows_j = slice(32 * (j % 4), 32 * (j % 4) + 32)
                for b in range(B):
                    for hq in range(NH // 4):
                        c0 = HS * (b % 2) + 4 * HD * hq
                        hf, q = divmod(hq, 4)
                        ins = pe.matmul(bank[b // 2][rows_j, c0:c0 + 4 * HD],
                                        A[:, j % 2, q, GT * (B * hf + b):GT * (B * hf + b) + GT],
                                        sgpad[:, j % 2, b, hq, :, :].rearrange("p h d -> p (h d)"),
                                        start=False, stop=False, skip_group_check=True)
                ins.then_inc(S_["z"], 1)

            def half_end(u):
                pe.wait_ge(S_["b_saved"], 64 * (u + 1))
                for k in range(2):
                    pe.matmul(bank[k][:, :], sel, biasr[:, u, 512 * k:512 * k + 512],
                              start=False, stop=True, skip_group_check=True).then_inc(S_["zh"], 1)

            def post_channels(f):
                pe.wait_ge(S_["yn"], f + 1)
                if f >= 2:
                    pe.wait_ge(S_["res"], f - 1)
                for k in range(KC):
                    ins = pe.transpose(bank[f_bank(f)][:, P * k:P * k + P], yn[:, f // 4, f % 4, P * k:P * k + P], ident)
                ins.then_inc(S_["yTp"], 1)

            def project(f):
                pe.wait_ge(S_["yT"], 2 * (f + 1))
                for k in range(KC):
                    ins = pe.matmul(bank[f_bank(f)][:, 256:512], yT[:, f % 2, k, :], wo[:, k, :],
                                    start=(k == 0), stop=(k == KC - 1))
                ins.then_inc(S_["o"], 1)

            xn_channels(0)
            pe.wait_ge(S_["wkv"], 16)
            pe.wait_ge(S_["xnTc"], 2)
            channels(wk, 0, 0, "kch")
            pe.wait_ge(S_["wlr"], 16)
            rates(0)
            pe.wait_ge(S_["kchc"], 2)
            pe.wait_ge(S_["wt"], 1)
            pair_rows(0, bank[6]).then_inc(S_["pair0"], 1)
            pe.wait_ge(S_["pair0T"], 1)
            xn_channels(1)
            pe.wait_ge(S_["wq"], 16)
            channels(wq, 0, 0, "qch")
            pe.wait_ge(S_["xnTc"], 4)
            rates(1)
            tile(0, 0)
            pe.wait_ge(S_["qchc"], 2)
            channels(wk, 0, 1, "kch")
            tile(0, 1)
            query_rows(0)
            tile(0, 2)
            pe.wait_ge(S_["kchc"], 4)
            channels(wq, 0, 1, "qch")
            tile(0, 3)
            pe.wait_ge(S_["wrt"], 16)
            pe.wait_ge(S_["xnTc"], 8)
            pe.wait_ge(S_["etaT"], 2)
            for f in range(NF):
                u, b = divmod(f, B)
                for k in range(KC):
                    ins = pe.matmul(bank[7][:, 256 + f * NE:256 + (f + 1) * NE], xnL[:, k, b, P * u:P * u + P],
                                    wrt[:, k, :], start=(k == 0), stop=(k == KC - 1))
            ins.then_inc(S_["route"], 1)
            query_rows(1)
            tile(0, 4)
            tile(1, 0)
            slot = 0
            for j in range(1, NG):
                last = slot + SLOTS[j]
                tile(j, 1)
                tile(j, 2)
                expert_slot(slot)
                if j != 5:
                    group_start(j - 1)
                tile(j, 3)
                expert_slot(slot + 1)
                tile(j, 4)
                for i in range(slot + 2, last):
                    expert_slot(i)
                if j == 5:
                    group_start(4)
                group_end(j - 1)
                if j == 4:
                    half_end(0)
                if j + 2 < NG:
                    tile(j + 1, 0)
                slot = last
            group_start(NG - 1)
            pe.wait_ge(S_["wo"], 16)
            pe.wait_ge(S_["tile_done"], 5 * NG - 1)
            for i in range(slot, NS + 2):
                expert_slot(i)
                if i == slot + 2:
                    group_end(NG - 1)
                    half_end(1)
                if i > FIRST:
                    project(i - 1 - FIRST)
                if i >= FIRST:
                    post_channels(i - FIRST)
            project(NF - 1)


def kernel(**inputs):
    import numpy as np
    import concourse.bacc as bacc
    from concourse.bass_utils import run_bass_kernel_spmd

    a = {k: np.ascontiguousarray(w) for k, w in inputs.items()}

    def in_major(w):
        return w.T.reshape(KC, P, -1).transpose(1, 0, 2)

    def rep(w):
        return np.broadcast_to(w.reshape(1, -1), (P, w.size))

    def pairs(w):
        return np.broadcast_to(w.reshape(1, NH, -1), (B, NH, w.size // NH)).reshape(P, -1)

    def half_tiles(x):
        return x.reshape(B, 2, P, HS).transpose(2, 1, 0, 3).reshape(P, NF, HS)

    x = a["L0_attn_hidden_states"]
    gu = a["L0_ffn_expert_gate_up"].reshape(NE, KC, P, NI, 2).transpose(2, 1, 0, 4, 3).reshape(P, KC, NE, 2 * NI)
    p = np.arange(P)
    s, t = p[:, None] % GT, np.arange(GT)[None, :]
    parts = {
        "gam": pairs(a["L0_attn_ttt_norm_weight"]), "bet": pairs(a["L0_attn_ttt_norm_bias"]),
        "w0": np.concatenate([pairs(a["L0_attn_W1"]), pairs(a["L0_attn_b1"])], 1),
        "lrb": pairs(a["L0_attn_ttt_lr_bias"]),
        "gam_row": rep(a["L0_attn_ttt_norm_weight"]), "bet_row": rep(a["L0_attn_ttt_norm_bias"]),
        "lti": rep(a["L0_attn_learnable_token_idx"]), "inv": rep(1.0 / np.arange(1, K + 1)),
        "iota": rep(np.arange(NE)), "hmask": p[:, None] // GT == np.arange(4)[None, :],
        "cmask": p[:, None] // HD % 4 == np.arange(4)[None, :],
        "mask_tok": ((s // K == t // K) & (s <= t)) * (-1.0 / HD), "mask_last": (s // K < t // K) * (-1.0 / HD),
        "post_w": a["L0_attn_post_norm_weight"].reshape(KC, P).T,
        "post_b": a["L0_attn_post_norm_bias"].reshape(KC, P).T,
        "ident": np.eye(P), "sel": p[:, None] == p[None, :] // GT,
    }
    arrays = {
        "x_bt": x.reshape(B, NG, GT, HS).transpose(0, 2, 1, 3).reshape(P, NG, HS), "x_tok": half_tiles(x),
        "small": np.concatenate([np.asarray(parts[k], np.float32) for k in SMALL], 1),
        "wkv": np.stack([in_major(a["L0_attn_k_w"]), in_major(a["L0_attn_v_w"])], 1),
        "wq": in_major(a["L0_attn_q_w"]),
        "wlr": in_major(a["L0_attn_ttt_lr_weight"].reshape(NH, HS)), "wrt": in_major(a["L0_ffn_router_gate"]),
        "gup": gu, "down": a["L0_ffn_expert_down"].transpose(1, 0, 2), "wo": in_major(a["L0_attn_o_w"]),
    }
    arrays = {f"in_{k}": np.ascontiguousarray(w, dtype=np.float32) for k, w in arrays.items()}
    nc = bacc.Bacc("TRN2", target_bir_lowering=False, num_devices=1)
    aps = [nc.dram_tensor(k, w.shape, F32, kind="ExternalInput").ap() for k, w in arrays.items()]
    out = nc.dram_tensor("out", (P, NF, HS), F32, kind="ExternalOutput").ap()
    build(nc, *aps, out)
    r = run_bass_kernel_spmd(nc, [arrays], core_ids=[0])
    return r.results[0]["out"].reshape(P, 2, B, HS).transpose(2, 1, 0, 3).reshape(B, L, HS)
```

```python
import concourse.bass as bass
from concourse import mybir
from contextlib import ExitStack

F32 = mybir.dt.float32
U32 = mybir.dt.uint32
ALU = mybir.AluOpType
ACT = mybir.ActivationFunctionType
AX = mybir.AxisListType

P = 128
B, L, HS = 4, 256, 256
NH, HD, K = 32, 8, 16
NG = 8
GT = L // NG
KC = HS // P
HH = P // HD
C1 = HD + 1
NE, NI = 8, 128
NF = 2 * B
NS = NF * NE // 2
FIRST_HALF = [0, 3, 2, 3, 3, 3, 4, 4]
SLOTS = [0, 3, 4, 4, 4, 4, 5, 5]
SMALL_WIDTHS = dict(gam=HD, bet=HD, w0=C1 * HD, lrb=1, gam_row=HS, bet_row=HS, lti=K, inv=K, iota=NE, bmask=4,
                    cmask=4, mask_tok=GT, mask_last=GT, post_w=KC, post_b=KC, ident=P, sel=P)
SMALL, SMALL_N = {}, 0
for name, width in SMALL_WIDTHS.items():
    SMALL[name] = (SMALL_N, width)
    SMALL_N += width
EPS, EPS_IN = 1e-6, 1e-5
F32R = mybir.dt.float32r
TOP = 0xFFFFF000
BR = P + 1


def build(nc, x_bt_d, x_tok_d, small_d, wkv_d, wq_d, wlr_d, wrt_d, gup_d, down_d, wo_d, out_d):
    wblk_d = nc.dram_tensor("w_blocks", [B * KC * BR, P], F32, kind="Internal")

    with ExitStack() as ctx:
        def sb(name, shape, dt=F32):
            return ctx.enter_context(nc.sbuf_tensor(name, shape, dt))

        def sem(name):
            return ctx.enter_context(nc.semaphore(name))

        bank = [ctx.enter_context(nc.psum_tensor(f"bank{i}", [P, 512], F32)) for i in range(8)]

        x_bt = sb("x_bt", [P, NG, HS])
        small = sb("small", [P, SMALL_N])
        wkv = sb("wkv", [P, 2, KC, HS])
        wq = sb("wq", [P, KC, HS])
        wo = sb("wo", [P, KC, HS])
        wlr = sb("wlr", [P, KC, NH])
        wrt = sb("wrt", [P, KC, NE])
        gup_hi = sb("gup_hi", [P, KC, NE, 2 * NI])
        gup_lo = sb("gup_lo", [P, KC, NE, 2 * NI])
        down = sb("down", [P, NE, HS])
        wk, wv = wkv[:, 0], wkv[:, 1]

        def part(name):
            a, n = SMALL[name]
            return small[:, a:a + n]

        ident, bmask, cmask, mask_tok, mask_last, iota, inv, lti = (
            part(k) for k in ("ident", "bmask", "cmask", "mask_tok", "mask_last", "iota", "inv", "lti"))
        sel = small[0:4, SMALL["sel"][0]:SMALL["sel"][0] + P]
        gam_row, bet_row = part("gam_row"), part("bet_row")
        gam, bet, w0, lrb = part("gam"), part("bet"), part("w0"), part("lrb")
        post_w, post_b = part("post_w"), part("post_b")

        xn = sb("xn", [P, NG, HS])
        xnT = sb("xnT", [P, KC, NG, P])
        xnL_hi = sb("xnL_hi", [P, KC, B, L])
        xnL_lo = sb("xnL_lo", [P, KC, B, L])
        ones_row = sb("ones_row", [1, P])
        eps_in = sb("eps_in", [P, 1])
        eps = sb("eps", [P, 1])
        one = sb("one", [P, 1])
        stats = sb("stats", [P, NG, 6])
        mv = sb("mv", [P, NG, 2])
        std_in = sb("std_in", [P, NG])
        rstd_in = sb("rstd_in", [P, NG])
        wt = sb("wt", [P, KC, HS])
        wtree = sb("wtree", [P, KC * HS // 2])
        grow = sb("grow", [P, HS])
        growtree = sb("growtree", [P, HS // 2])
        tok = sb("tok", [P, K])
        ntok = sb("ntok", [P, 1])
        mask = sb("mask", [P, GT])
        mask2 = sb("mask2", [P, GT])
        g2 = sb("g2", [P, HD])

        xkT = sb("xkT", [P, KC, NG, P])
        xqT = sb("xqT", [P, KC, B, L])
        xqm = sb("xqm", [P, 2, KC, B, 4, GT])
        KP = sb("KP", [P, 2, C1, GT])
        QP = sb("QP", [P, 2, HD, GT])
        eta = sb("eta", [P, NG * GT])
        sig = sb("sig", [P, NG * GT])

        W = sb("W", [P, 2, C1 * HD])
        wmean = sb("wmean", [P, C1])
        pr1 = sb("pr1", [P, HD * K * C1])
        pr2 = sb("pr2", [P, C1 * HD * K])
        T = sb("T", [P, 5, HD * K])
        S = sb("S", [P, 3, K])
        sxx = sb("sxx", [P, K])
        var = sb("var", [P, K])
        rr = sb("rr", [P, 2, K])
        rs = sb("rs", [P, 2, K])
        a3 = sb("a3", [P, 2, K])
        cf = sb("cf", [P, 4, K])
        hb = sb("hb", [P, 5, HD * K])
        sgb = sb("sgb", [P, HD, GT])
        sgT = sb("sgT", [P, HS])
        sgpad = sb("sgpad", [P, 2, NH, B, HD])
        dW = sb("dW", [P, C1 * HD])
        A = sb("A", [P, 2, 4, KC * B * GT])
        wblk = sb("wblk", [P, 2, B * KC, P])

        mx = sb("mx", [P, NF, 8])
        mi = sb("mi", [P, NF, 8], U32)
        mif = sb("mif", [P, NF, 2])
        gap = sb("gap", [P, NF])
        s12 = sb("s12", [P, 2, NF])
        oh = sb("oh", [P, 2, NF, NE])
        wexp = sb("wexp", [P, NF, NE])
        gate = sb("gate", [P, 2, 2, NI])
        upw = sb("upw", [P, 2, 2, NI])
        hh = sb("hh", [P, 2, 2, NI])
        hT = sb("hT", [P, 2, 2, P])
        G = sb("G", [P, NF, HS])
        pe_warm = sb("pe_warm", [P, 256])
        warm = sb("warm", [P, 2 * NG])

        xqb = sb("xqb", [P, 2, B, HS])
        zc = x_bt[:, :, :].rearrange("p (u b) c -> p u (b c)", u=2)
        yn = xn[:, :, :].rearrange("p (u b) c -> p u b c", u=2)
        biasr = xn[0:4, :, :].rearrange("p (u b) c -> p u (b c)", u=2)
        x_tok = xkT[:, :, :, :].rearrange("p k j t -> p (k j t)").rearrange("p (f c) -> p f c", c=HS)
        zsq = wkv[:, :, :, :].rearrange("p w k c -> p w (k c)")
        zg = sb("zg", [P, 2, 512])
        zv = sb("zv", [P, 2, 64])
        zs = sb("zs", [P, 2, 64])
        zr = sb("zr", [P, 2, 64])
        o = zg
        ostat = sb("ostat", [P, B, 6])
        omv = sb("omv", [P, B, 2])
        osd = sb("osd", [P, B])
        ors = sb("ors", [P, B])
        yT = sb("yT", [P, 2, KC, P])

        def flat(a):
            return a.rearrange("p a b c -> p (a b c)") if len(a.shape) == 4 else a.rearrange("p a b -> p (a b)")

        sgpad_flat = sgpad[:, :, :, :, :].rearrange("p r h b d -> p (r h b d)")
        gup = (sgpad_flat, flat(G[:, :, :]))
        xnL = sgpad_flat.rearrange("p (k b t) -> p k b t", k=KC, b=B)
        top = flat(x_bt[:, :, :])
        splits = [(gup[0], flat(gup_hi[:, 0]), flat(gup_lo[:, 0])), (gup[1], flat(gup_hi[:, 1]), flat(gup_lo[:, 1])),
                  (sgpad_flat, flat(xnL_hi[:, :, :, :]), flat(xnL_lo[:, :, :, :]))]

        names = """warm x_a x_b small wkv wq wlr wrt gup0 gup1 down wo xt
            dve0 pool0 var std xn xnT xnTc kch kchc qch qchc eta etaT sig wt
            pair0 pair0T rows rowsc xqb route gap s12 wx rdve
            zero_w zero_d top hi split queries pair pair_done sc scored mask masked chain vrc rstd sg w w_saved w_loaded b_saved
            sgT sgp z0 z zc gu gact h hTp hT y g
            zg zv zs post0 ov os yn yTp yT o res fin out"""
        S_ = {n: sem("s_" + n) for n in names.split()}

        block = ctx.enter_context(nc.Block())

        def f_bank(f):
            return 2 + f % 4

        @block.sync
        def _(sp):
            sp.dma_start(x_bt[:, 0:4, :], x_bt_d[:, 0:4, :]).then_inc(S_["x_a"], 16)
            sp.dma_start(x_bt[:, 4:8, :], x_bt_d[:, 4:8, :]).then_inc(S_["x_b"], 16)
            sp.dma_start(wq[:, :, :], wq_d).then_inc(S_["wq"], 16)
            sp.dma_start(wrt[:, :, :], wrt_d).then_inc(S_["wrt"], 16)
            for k in range(KC):
                sp.dma_start(gup[k], gup_d[:, k]).then_inc(S_[f"gup{k}"], 16)
            sp.wait_ge(S_["zero_w"], 1)
            sp.dma_start(bass.AP(wblk_d, 0, [[P, P], [BR * P, B * KC], [1, P]]), wblk[:, 0, :, :]).then_inc(S_["zero_d"], 16)
            sp.dma_start(down[:, :, :], down_d).then_inc(S_["down"], 16)
            sp.dma_start(wo[:, :, :], wo_d).then_inc(S_["wo"], 16)
            sp.wait_ge(S_["zero_d"], 16)

            def save_w(j):
                sp.wait_ge(S_["w"], 2 * j + 1)
                if j:
                    sp.wait_ge(S_["w_loaded"], 16 * j)
                sp.dma_start(bass.AP(wblk_d, 0, [[HD * P + HD, P], [P, HD], [1, HD]]),
                             W[:, 0, 0:HD * HD].rearrange("p (c d) -> p c d", d=HD)).then_inc(S_["w_saved"], 16)

            def load_w(j):
                sp.wait_ge(S_["w_saved"], 16 * (j + 1))
                if j >= 2:
                    sp.wait_ge(S_["z0"], j - 1)
                sp.dma_start(wblk[:, j % 2, :, :],
                             bass.AP(wblk_d, 0, [[P, P], [BR * P, B * KC], [1, P]])).then_inc(S_["w_loaded"], 16)

            def save_b(j):
                if j:
                    sp.wait_ge(S_["b_saved"], 64 * j)
                else:
                    sp.wait_ge(S_["xnT"], 4)
                for b in range(B):
                    sp.dma_start(biasr[j % 4:j % 4 + 1, j // 4, :].rearrange("p (h b d) -> p b h d", b=B, d=HD)[:, b],
                                 W[b * NH:b * NH + NH, 0, HD * HD:]).then_inc(S_["b_saved"], 16)

            save_w(0)
            load_w(0)
            save_b(0)
            for j in range(NG):
                if j + 1 < NG:
                    save_w(j + 1)
                if j + 1 < NG:
                    load_w(j + 1)
                if j + 1 < NG:
                    save_b(j + 1)
                if j == 7:
                    sp.wait_ge(S_["sc"], 4 * NG)
                    sp.dma_start(x_tok[:, :, :], x_tok_d).then_inc(S_["xt"], 16)
            for f in range(0, NF, 2):
                sp.wait_ge(S_["fin"], f + 2)
                sp.dma_start(out_d[:, f:f + 2, :], G[:, f:f + 2, :]).then_inc(S_["out"], 16)
            sp.wait_ge(S_["out"], 16 * NF // 2)

        @block.gpsimd
        def _(pool):
            mask_bc = mask[:, :].unsqueeze(1).broadcast_to([P, KC * B, GT])

            def mask_scores(j, i):
                pool.wait_ge(S_["scored"], 4 * j + i)
                scores = A[:, j % 2, i - 1, :].rearrange("p (h t) -> p h t", t=GT)
                pool.tensor_tensor(scores, scores, mask_bc, ALU.mult).then_inc(S_["masked"], 1)

            pool.memset(pe_warm[:, :], 0.0).then_inc(S_["warm"], 1)
            pool.memset(ones_row[:, :], 1.0).then_inc(S_["pool0"], 1)
            pool.memset(KP[:, :, HD, :], 1.0).then_inc(S_["pool0"], 1)
            n = [2]

            def link(ins):
                n[0] += 1
                ins.then_inc(S_["pool0"], 1)
                pool.wait_ge(S_["pool0"], n[0])

            def centre(full, tree, m):
                v = full.rearrange("p (m d) -> p m d", d=HD)
                t4 = tree.rearrange("p (m d) -> p m d", d=4)
                link(pool.tensor_tensor(t4, v[:, :, 0:4], v[:, :, 4:8], ALU.add))
                link(pool.tensor_tensor(t4[:, :, 0:2], t4[:, :, 0:2], t4[:, :, 2:4], ALU.add))
                link(pool.tensor_tensor(t4[:, :, 0:1], t4[:, :, 0:1], t4[:, :, 1:2], ALU.add))
                link(pool.tensor_scalar(t4[:, :, 0:1], t4[:, :, 0:1], -1.0 / HD, 0.0, ALU.mult, ALU.add))
                return pool.tensor_tensor(v, v, t4[:, :, 0:1].broadcast_to([P, m, HD]), ALU.add)

            pool.wait_ge(S_["small"], 16)
            link(pool.tensor_tensor(grow[:, :], gam_row, bet_row, ALU.mult))
            link(centre(grow[:, :], growtree[:, :], NH))
            pool.wait_ge(S_["wkv"], 16)
            link(pool.tensor_tensor(wt[:, :, :], wk, wv, ALU.subtract))
            link(pool.tensor_tensor(wt[:, :, :], wt[:, :, :], gam_row.unsqueeze(1).broadcast_to([P, KC, HS]), ALU.mult))
            centre(wt[:, :, :].rearrange("p a b -> p (a b)"), wtree[:, :], KC * NH).then_inc(S_["wt"], 1)
            pool.memset(wblk[:, 0, :, :], 0.0).then_inc(S_["zero_w"], 1)

            def masked_queries(j):
                pool.wait_ge(S_["qchc"], 2 + 2 * (j // 4))
                if j >= 2:
                    pool.wait_ge(S_["sc"], 4 * (j - 1))
                for h in range(4):
                    pool.tensor_scalar(xqm[:, j % 2, :, :, h, :], xqT[:, :, :, GT * j:GT * j + GT],
                                       cmask[:, h:h + 1], 0.0, ALU.mult, ALU.add).then_inc(S_["queries"], 1)

            def hidden_product(i):
                pool.wait_ge(S_["gact"], 3 * (i + 1))
                if i >= 2:
                    pool.wait_ge(S_["hTp"], i - 1)
                pool.tensor_tensor(hh[:, i % 2, :, :], gate[:, i % 2, :, :], upw[:, i % 2, :, :],
                                   ALU.mult).then_inc(S_["h"], 1)

            def half_scale(u):
                for k in range(2):
                    pool.wait_ge(S_["zc"], 4 * u + 4)
                    if u:
                        pool.wait_ge(S_["yn"], 2 * (k + 1))
                    pool.tensor_tensor(zg[:, k, :].rearrange("p (b c) -> p b c", c=HS),
                                       zc[:, u, 512 * k:512 * k + 512].rearrange("p (b c) -> p b c", c=HS),
                                       gam_row.unsqueeze(1).broadcast_to([P, 2, HS]), ALU.mult).then_inc(S_["zg"], 1)

            def pad_grads(j):
                pool.wait_ge(S_["sgT"], j + 1)
                if j >= 2:
                    pool.wait_ge(S_["z"], 2 * (j - 1))
                for hf in range(KC):
                    heads = slice(HH * hf, HH * hf + HH)
                    pool.tensor_tensor(sgpad[:, j % 2, heads, :, :],
                                       sgT[:, :].rearrange("p (h d) -> p h d", d=HD)[:, heads].unsqueeze(2)
                                       .broadcast_to([P, HH, B, HD]),
                                       bmask.unsqueeze(1).unsqueeze(3).broadcast_to([P, HH, B, HD]),
                                       ALU.mult).then_inc(S_["sgp"], 1)

            def residual(f):
                pool.wait_ge(S_["res"], f + 1)
                pool.tensor_tensor(G[:, f, :], G[:, f, :], x_tok[:, f, :], ALU.add).then_inc(S_["fin"], 1)

            def lower_half(n):
                full, _, lo = splits[n]
                pool.wait_ge(S_["top"], n + 1)
                pool.tensor_tensor(lo.bitcast(F32R), full, top, ALU.subtract).then_inc(S_["split"], 1)

            lower_half(0)
            masked_queries(0)
            masked_queries(1)
            pool.wait_ge(S_["mask"], 1)
            lower_half(1)
            for i in range(1, 4):
                mask_scores(0, i)
            lower_half(2)
            mask_scores(0, 4)
            pool.wait_ge(S_["route"], 1)
            slot = 0
            for j in range(NG):
                if 1 < j + 1 < NG:
                    masked_queries(j + 1)
                if j == 1:
                    pool.wait_ge(S_["rowsc"], 4)
                    for u in range(2):
                        pool.tensor_tensor(xqb[:, u, :, :], xqb[:, u, :, :],
                                           bet_row.unsqueeze(1).broadcast_to([P, B, HS]), ALU.add).then_inc(S_["xqb"], 1)
                if j == 6:
                    half_scale(0)
                if not j:
                    continue
                mask_scores(j, 1)
                hidden_product(slot)
                mask_scores(j, 2)
                pad_grads(j - 1)
                mask_scores(j, 3)
                hidden_product(slot + 1)
                mask_scores(j, 4)
                for i in range(slot + 2, slot + SLOTS[j]):
                    hidden_product(i)
                slot += SLOTS[j]
            pad_grads(NG - 1)
            for i in range(slot, NS):
                hidden_product(i)
                if i == slot:
                    half_scale(1)
            pool.wait_ge(S_["xt"], 16)
            for f in range(NF):
                residual(f)

        @block.scalar
        def _(act):
            act.dma_start(small[:, :], small_d).then_inc(S_["small"], 16)
            act.dma_start(wkv[:, :, :, :], wkv_d).then_inc(S_["wkv"], 16)
            act.dma_start(wlr[:, :, :], wlr_d).then_inc(S_["wlr"], 16)

            def input_std(u):
                act.wait_ge(S_["var"], u + 1)
                if u == 0:
                    act.wait_ge(S_["dve0"], 3)
                act.activation(std_in[:, 4 * u:4 * u + 4], mv[:, 4 * u:4 * u + 4, 1], ACT.Sqrt,
                               bias=eps_in[:, 0:1]).then_inc(S_["std"], 1)

            def xn_out(u):
                for k in range(KC):
                    i = 2 * u + k
                    act.wait_ge(S_["xnT"], i + 1)
                    act.copy(xnT[:, k, 4 * u:4 * u + 4, :].rearrange("p j t -> p (j t)"), bank[4 + i][:, :]).then_inc(S_["xnTc"], 1)

            def keys_out(n, bk, first, end):
                for hf in range(KC):
                    act.wait_ge(S_["kch"], 2 * n + hf + 1)
                    act.copy(xkT[:, hf, first:end, :].rearrange("p j t -> p (j t)"),
                             bank[bk + hf][:, P * (first % 4):P * (first % 4) + P * (end - first)]).then_inc(S_["kchc"], 1)

            def queries_out(u):
                for hf in range(KC):
                    act.wait_ge(S_["qch"], 2 * u + hf + 1)
                    act.copy(xqT[:, hf, :, P * u:P * u + P].rearrange("p b (j t) -> p j b t", t=GT),
                             bank[hf][:, :].rearrange("p (j b t) -> p j b t", j=4, b=B)).then_inc(S_["qchc"], 1)

            def rates(u):
                act.wait_ge(S_["etaT"], u + 1)
                act.activation(sig[:, P * u:P * u + P], eta[:, P * u:P * u + P], ACT.Sigmoid,
                               bias=lrb).then_inc(S_["sig"], 1)

            def query_rows(u):
                for i in range(2 * u, 2 * u + 2):
                    act.wait_ge(S_["rows"], i + 1)
                    act.copy(xqb[:, u, :, P * (i % 2):P * (i % 2) + P],
                             bank[4 + i % 2][:, :].rearrange("p (b c) -> p b c", b=B)).then_inc(S_["rowsc"], 1)

            def high_half(n):
                act.wait_ge(S_["top"], n + 1)
                act.copy(splits[n][1].bitcast(F32R), top).then_inc(S_["hi"], 1)

            def scores_out(j, i):
                act.wait_ge(S_["sc"], 4 * j + i)
                act.activation(A[:, j % 2, i - 1, :], bank[2 + (j + i) % 2][:, 0:256], ACT.Identity,
                               bias=one[:, 0:1]).then_inc(S_["scored"], 1)

            def step_std(n):
                act.wait_ge(S_["vrc"], n + 1)
                act.activation(rr[:, 0, :], rr[:, 1, :], ACT.Sqrt).then_inc(S_["rstd"], 1)

            def expert_slot(i):
                f, e = divmod(i, 4)
                if i < NS:
                    bk = bank[4 + i % 2][:, :].rearrange("p (e g i) -> p e g i", e=2, g=2)
                    act.wait_ge(S_["gu"], i + 1)
                    if i >= 2:
                        act.wait_ge(S_["h"], i - 1)
                    act.activation(gate[:, i % 2, :, :], bk[:, :, 0, :], ACT.Silu).then_inc(S_["gact"], 1)
                    for r in range(2):
                        act.activation(upw[:, i % 2, r, :], bk[:, r, 1, :], ACT.Copy,
                                       scale=wexp[:, f, 2 * e + r:2 * e + r + 1]).then_inc(S_["gact"], 1)
                if 1 <= i <= NS:
                    act.wait_ge(S_["hTp"], i)
                    if i >= 3:
                        act.wait_ge(S_["y"], i - 2)
                    act.copy(hT[:, (i - 1) % 2, :, :].rearrange("p e t -> p (e t)"), bank[6][:, 0:2 * P]).then_inc(S_["hT"], 1)
                if i >= 5 and e == 1:
                    act.wait_ge(S_["y"], i - 1)
                    act.activation(G[:, f - 1, :], bank[7][:, 0:HS], ACT.Silu).then_inc(S_["g"], 1)

            def preload_sqrt(n):
                act.activation(warm[:, n:n + 1], eps[:, :], ACT.Sqrt)

            def half_out(u):
                if u:
                    act.wait_ge(S_["zv"], 2)
                views = (zsq.rearrange("p w (k h d) -> p (w k) h d", k=2, d=HD),
                         x_bt[:, 4 * u:4 * u + 4, :].rearrange("p b (h d) -> p b h d", d=HD))
                for view, func in zip(views, (ACT.Square, ACT.Copy)):
                    for k in range(2):
                        if func == ACT.Square:
                            act.wait_ge(S_["z"], 8 * u + 6 + k + 1)
                        act.activation(view[:, :, HH * k:HH * k + HH, :].rearrange("p b h d -> p h b d"),
                                       bank[k][:, :].rearrange("p (h b d) -> p h b d", b=B, d=HD), func
                                       ).then_inc(S_["zc"], 1)

            def norm_z(u):
                for k in range(2):
                    act.wait_ge(S_["zv"], 2 * u + k + 1)
                    act.activation(zs[:, k, :], zv[:, k, :], ACT.Sqrt, bias=eps[:, 0:1], scale=1.0 / HD).then_inc(S_["zs"], 1)

            def norm_o(u):
                for k in range(2):
                    act.wait_ge(S_["ov"], 2 * u + k + 1)
                    act.activation(osd[:, 2 * k:2 * k + 2], omv[:, 2 * k:2 * k + 2, 1], ACT.Sqrt,
                                   bias=eps[:, 0:1]).then_inc(S_["os"], 1)

            def post_rows(f):
                act.wait_ge(S_["yTp"], f + 1)
                if f >= 2:
                    act.wait_ge(S_["o"], f - 1)
                for k in range(KC):
                    act.activation(yT[:, f % 2, k, :], bank[f_bank(f)][:, P * k:P * k + P], ACT.Identity,
                                   scale=post_w[:, k:k + 1], bias=post_b[:, k:k + 1]).then_inc(S_["yT"], 1)

            input_std(0)
            input_std(1)
            xn_out(0)
            keys_out(0, 2, 0, 1)
            rates(0)
            keys_out(1, 0, 1, 4)
            preload_sqrt(0)
            step_std(0)
            queries_out(0)
            high_half(0)
            xn_out(1)
            keys_out(2, 0, 4, 8)
            scores_out(0, 1)
            scores_out(0, 2)
            step_std(1)
            scores_out(0, 3)
            act.wait_ge(S_["split"], 1)
            for k in range(KC):
                for u in range(2):
                    act.copy(xnL[:, k, :, P * u:P * u + P].rearrange("p b (j t) -> p j b t", t=GT),
                             xnT[:, k, 4 * u:4 * u + 4, :].rearrange("p j (b t) -> p j b t", b=B)).then_inc(S_["xnTc"], 1)
            query_rows(0)
            scores_out(0, 4)
            high_half(1)
            queries_out(1)
            step_std(2)
            high_half(2)
            query_rows(1)
            rates(1)
            act.wait_ge(S_["gap"], 1)
            act.activation(s12[:, 0, :], gap[:, :], ACT.Sigmoid).then_inc(S_["s12"], 1)
            act.activation(s12[:, 1, :], gap[:, :], ACT.Sigmoid, scale=-1.0).then_inc(S_["s12"], 1)
            preload_sqrt(1)
            scores_out(1, 1)
            step_std(3)
            slot = 0
            for j in range(1, NG):
                if j > 2:
                    step_std(2 * j)
                if j == 5:
                    half_out(0)
                scores_out(j, 2)
                if j == 1:
                    act.wait_ge(S_["wx"], 1)
                    expert_slot(0)
                scores_out(j, 3)
                expert_slot(slot + 1)
                scores_out(j, 4)
                for i in range(slot + 2, slot + FIRST_HALF[j]):
                    expert_slot(i)
                if j > 1:
                    preload_sqrt(2 * j)
                    step_std(2 * j + 1)
                for i in range(slot + FIRST_HALF[j], slot + SLOTS[j]):
                    expert_slot(i)
                slot += SLOTS[j]
                if j == 1:
                    preload_sqrt(3)
                    step_std(4)
                if j + 1 < NG:
                    scores_out(j + 1, 1)
                    expert_slot(slot)
                if 1 < j < NG - 1:
                    preload_sqrt(2 * j + 1)
            norm_z(0)
            expert_slot(slot)
            half_out(1)
            norm_o(0)
            norm_z(1)
            for i in range(slot + 1, NS):
                expert_slot(i)
            post_rows(0)
            expert_slot(NS)
            post_rows(1)
            norm_o(1)
            post_rows(2)
            post_rows(3)
            expert_slot(NS + 1)
            for f in range(4, NF):
                post_rows(f)

        @block.vector
        def _(v):
            n0 = [0]

            def link(ins, semaphore=S_["dve0"], count=n0):
                count[0] += 1
                ins.then_inc(semaphore, 1)
                v.wait_ge(semaphore, count[0])

            link(v.memset(eps_in[:, :], EPS_IN))
            link(v.memset(eps[:, :], EPS))
            link(v.memset(one[:, :], 1.0))

            def input_stats(u):
                v.wait_ge(S_["x_b" if u else "x_a"], 16)
                for j in range(4 * u, 4 * u + 4):
                    ins = v.bn_stats(stats[:, j, :], x_bt[:, j, :])
                link(ins)
                for j in range(4 * u, 4 * u + 4):
                    ins = v.bn_aggr(mv[:, j, :], stats[:, j, :])
                ins.then_inc(S_["var"], 1)

            def input_norm(u):
                v.wait_ge(S_["std"], u + 1)
                link(v.reciprocal(rstd_in[:, 4 * u:4 * u + 4], std_in[:, 4 * u:4 * u + 4]))
                for j in range(4 * u, 4 * u + 4):
                    v.tensor_scalar(xn[:, j, :], x_bt[:, j, :], mv[:, j, 0:1], rstd_in[:, j:j + 1],
                                    ALU.subtract, ALU.mult).then_inc(S_["xn"], 1)

            input_stats(0)
            input_stats(1)
            input_norm(0)
            v.wait_ge(S_["small"], 16)
            link(v.tensor_tensor(g2[:, :], gam, gam, ALU.mult))
            link(v.tensor_reduce(wmean[:, :], w0.rearrange("p (c d) -> p c d", d=HD), AX.X, ALU.add))
            link(v.tensor_scalar(wmean[:, :], wmean[:, :], -1.0 / HD, None, ALU.mult))
            v.tensor_tensor(W[:, 0, :].rearrange("p (c d) -> p c d", d=HD), w0.rearrange("p (c d) -> p c d", d=HD),
                            wmean[:, :].unsqueeze(2).broadcast_to([P, C1, HD]), ALU.add).then_inc(S_["w"], 1)
            link(v.tensor_tensor(tok[:, :], inv, lti, ALU.add))
            link(v.tensor_scalar(tok[:, :], tok[:, :], 0.0, None, ALU.max))
            input_norm(1)
            link(v.tensor_scalar(ntok[:, :], tok[:, K - 1:K], -1.0 / HD, None, ALU.mult))
            link(v.tensor_tensor(mask[:, :].rearrange("p (m t) -> p m t", t=K),
                                 mask_tok.rearrange("p (m t) -> p m t", t=K),
                                 tok[:, :].unsqueeze(1).broadcast_to([P, 2, K]), ALU.mult))
            link(v.tensor_scalar(mask2[:, :], mask_last, tok[:, K - 1:K], None, ALU.mult))
            v.tensor_tensor(mask[:, :], mask[:, :], mask2[:, :], ALU.add).then_inc(S_["mask"], 1)

            def rates_to_pairs(u):
                v.wait_ge(S_["eta"], u + 1)
                v.transpose(eta[:, P * u:P * u + P], bank[7][:, P * u:P * u + P]).then_inc(S_["etaT"], 1)

            def group_to_pairs(ring, bk):
                v.transpose(KP[:, ring, 0:HD, :],
                            bk[:, 0:256].rearrange("p (h c) -> p c h", c=HD))
                return v.transpose(QP[:, ring, :, :],
                                   bk[:, 256:512].rearrange("p (h c) -> p c h", c=HD))

            r0 = [0]

            def route_gap():
                v.wait_ge(S_["route"], 1)
                logits = bank[6][:, 256:256 + NF * NE].rearrange("p (f e) -> p f e", e=NE)
                for f in range(NF):
                    ins = v.max(mx[:, f, :], logits[:, f, :])
                link(ins, S_["rdve"], r0)
                v.tensor_tensor(gap[:, :], mx[:, :, 0], mx[:, :, 1], ALU.subtract).then_inc(S_["gap"], 1)
                for f in range(NF):
                    ins = v.max_index(mi[:, f, :], mx[:, f, :], logits[:, f, :])
                link(ins, S_["rdve"], r0)
                link(v.tensor_copy(mif[:, :, :], mi[:, :, 0:2]), S_["rdve"], r0)

            def route_weights():
                for k in range(2):
                    link(v.tensor_tensor(oh[:, k, :, :], iota.unsqueeze(1).broadcast_to([P, NF, NE]),
                                         mif[:, :, k:k + 1].broadcast_to([P, NF, NE]), ALU.is_equal), S_["rdve"], r0)
                v.wait_ge(S_["s12"], 2)
                for k in range(2):
                    link(v.tensor_tensor(oh[:, k, :, :], oh[:, k, :, :],
                                         s12[:, k, :].unsqueeze(2).broadcast_to([P, NF, NE]), ALU.mult), S_["rdve"], r0)
                v.tensor_tensor(wexp[:, :, :], oh[:, 0, :, :], oh[:, 1, :, :], ALU.add).then_inc(S_["wx"], 1)

            OPS = 16

            def minibatch(j, ring, m, fill, last=False):
                n = j * 2 + m
                Wn = W[:, m, :]
                kp, qn = KP[:, ring, :, K * m:K * m + K], QP[:, ring, :, K * m:K * m + K]
                sg_n = sig[:, bass.ds(j * GT + K * m, K)]
                chain = S_["chain"]
                done = lambda k: v.wait_ge(chain, n * OPS + k)
                dt = lambda a: a.rearrange("p (d t) -> p d t", d=HD)
                b3 = lambda a: a.unsqueeze(1).broadcast_to([P, HD, K])
                x, u, pq, ux, xx = (dt(T[:, i, :]) for i in range(5))

                v.wait_ge(S_["w"], n + 1)
                if m == 0 and (not isinstance(j, int) or j):
                    v.wait_ge(S_["pair_done"], j)
                v.tensor_tensor(pr1[:, :].rearrange("p (d t c) -> p d t c", d=HD, t=K),
                                kp.rearrange("p c t -> p t c").unsqueeze(1).broadcast_to([P, HD, K, C1]),
                                Wn.rearrange("p (c d) -> p d c", d=HD).unsqueeze(2).broadcast_to([P, HD, K, C1]),
                                ALU.mult).then_inc(chain, 1)
                fill(0)
                done(1)
                v.tensor_reduce(T[:, 0, :], pr1[:, :].rearrange("p (a c) -> p a c", c=C1), AX.X,
                                ALU.add).then_inc(chain, 1)
                done(2)
                v.tensor_tensor(xx, x, x, ALU.mult).then_inc(chain, 1)
                v.tensor_tensor(u, x, g2[:, :].unsqueeze(2).broadcast_to([P, HD, K]), ALU.mult).then_inc(chain, 1)
                done(3)
                v.tensor_reduce(sxx[:, :], xx.rearrange("p d t -> p t d"), AX.X, ALU.add).then_inc(chain, 1)
                v.tensor_tensor(pq, x, qn, ALU.mult).then_inc(chain, 1)
                done(5)
                v.tensor_scalar(var[:, :], sxx[:, :], 1.0 / HD, EPS, ALU.mult, ALU.add).then_inc(chain, 1)
                v.tensor_tensor(ux, x, u, ALU.mult).then_inc(chain, 1)
                done(7)
                v.reciprocal(rr[:, 1, :], var[:, :]).then_inc(S_["vrc"], 1)
                done(8)
                v.tensor_reduce(S[:, :, :], T[:, 1:4, :].rearrange("p k (d t) -> p k t d", d=HD), AX.X,
                                ALU.add).then_inc(chain, 1)
                fill(1)
                v.wait_ge(S_["rstd"], n + 1)
                v.tensor_tensor(cf[:, 3:0:-2, :], rr[:, :, :], sg_n.unsqueeze(1).broadcast_to([P, 2, K]),
                                ALU.mult).then_inc(chain, 1)
                done(9)
                v.tensor_tensor(rs[:, :, :], rr[:, :, :], S[:, 1:3, :], ALU.mult).then_inc(chain, 1)
                done(10)
                v.tensor_tensor(dt(hb[:, 2, :]), qn, b3(cf[:, 3, :]), ALU.mult).then_inc(chain, 1)
                done(11)
                v.tensor_tensor(S[:, 1, :], rs[:, 0, :], rs[:, 1, :], ALU.add).then_inc(chain, 1)
                done(13)
                v.scalar_tensor_tensor(out=cf[:, 2::-2, :], in0=S[:, 0:2, :], scalar=-1.0 / HD,
                                       in1=cf[:, 1:2, :].broadcast_to([P, 2, K]),
                                       op0=ALU.mult, op1=ALU.mult).then_inc(chain, 1)
                done(14)
                v.tensor_tensor(hb[:, 0:2, :].rearrange("p k (d t) -> p k d t", d=HD),
                                T[:, 0:2, :].rearrange("p k (d t) -> p k d t", d=HD),
                                cf[:, 0:2, :].unsqueeze(2).broadcast_to([P, 2, HD, K]), ALU.mult).then_inc(chain, 1)
                v.tensor_tensor(dt(hb[:, 3, :]), dt(hb[:, 2, :]), b3(cf[:, 2, :]), ALU.add).then_inc(chain, 1)
                done(15)
                v.tensor_tensor(dt(hb[:, 4, :]), dt(hb[:, 0, :]), dt(hb[:, 1, :]), ALU.add).then_inc(S_["sg"], 1)
                v.wait_ge(S_["sg"], 4 * n + 1)
                sg = sgb[:, :, K * m:K * m + K]
                v.tensor_tensor(sg, dt(hb[:, 4, :]), dt(hb[:, 3, :]), ALU.add).then_inc(S_["sg"], 1)
                if last:
                    v.wait_ge(S_["sg"], 4 * n + 2)
                    return
                v.wait_ge(S_["sg"], 4 * n + 2)
                v.tensor_tensor(pr2[:, :].rearrange("p (c d t) -> p c d t", c=C1, d=HD),
                                kp.unsqueeze(2).broadcast_to([P, C1, HD, K]),
                                sg.unsqueeze(1).broadcast_to([P, C1, HD, K]), ALU.mult).then_inc(S_["sg"], 1)
                fill(2)
                v.wait_ge(S_["sg"], 4 * n + 3)
                v.tensor_reduce(dW[:, :], pr2[:, :].rearrange("p (a t) -> p a t", t=K), AX.X,
                                ALU.add).then_inc(S_["sg"], 1)
                if m == 1:
                    v.wait_ge(S_["w_saved"], 16 * (j + 1))
                    v.wait_ge(S_["b_saved"], 64 * (j + 1))
                v.wait_ge(S_["sg"], 4 * n + 4)
                v.scalar_tensor_tensor(out=W[:, 1 - m, :], in0=dW[:, :], scalar=ntok[:, 0:1], in1=Wn,
                                       op0=ALU.mult, op1=ALU.add).then_inc(S_["w"], 1)

            def upper_half(n):
                if n < 2:
                    v.wait_ge(S_[f"gup{n}"], 16)
                else:
                    v.wait_ge(S_["xnTc"], 8)
                if n:
                    v.wait_ge(S_["split"], n)
                    v.wait_ge(S_["hi"], n)
                v.tensor_scalar(top.bitcast(U32), splits[n][0].bitcast(U32), TOP, None, ALU.bitwise_and).then_inc(S_["top"], 1)

            def group(j, ring, between=None, late=None, last=False):
                def next_pairs(i):
                    if i == 0 and not last:
                        if isinstance(j, int) and j == 0:
                            upper_half(0)
                        v.wait_ge(S_["pair"], j + 1)
                        group_to_pairs(1 - ring, bank[2 + ring]).then_inc(S_["pair_done"], 1)
                    if i == 1 and isinstance(j, int) and j == 1:
                        upper_half(2)

                minibatch(j, ring, 0, next_pairs)
                if between:
                    between()
                minibatch(j, ring, 1, lambda i: late() if late and i == 1 else None, last)
                if not isinstance(j, int) or j:
                    v.wait_ge(S_["sgp"], 2 * j)
                v.transpose(sgT[:, :].rearrange("p (h d) -> p d h", d=HD),
                            sgb[:, :, :].rearrange("p d t -> p (d t)")).then_inc(S_["sgT"], 1)

            def half_variance(u):
                for k in range(2):
                    v.wait_ge(S_["zc"], 4 * u + 2)
                    v.tensor_reduce(zv[:, k, :], zsq[:, k, :].rearrange("p (a d) -> p a d", d=HD), AX.X,
                                    ALU.add).then_inc(S_["zv"], 1)

            def half_out_rows(u):
                p0 = post_count
                for k in range(2):
                    v.wait_ge(S_["zs"], 2 * u + k + 1)
                    link(v.reciprocal(zr[:, k, :], zs[:, k, :]), S_["post0"], p0)
                    v.wait_ge(S_["zg"], 2 * u + k + 1)
                    link(v.tensor_tensor(o[:, k, :].rearrange("p (a d) -> p a d", d=HD),
                                         zg[:, k, :].rearrange("p (a d) -> p a d", d=HD),
                                         zr[:, k, :].unsqueeze(2).broadcast_to([P, 64, HD]), ALU.mult), S_["post0"], p0)
                    v.wait_ge(S_["xqb"], 2)
                    link(v.tensor_tensor(o[:, k, :], o[:, k, :],
                                         xqb[:, u, 2 * k:2 * k + 2, :].rearrange("p b c -> p (b c)"), ALU.add), S_["post0"], p0)
                    for b in range(2):
                        ins = v.bn_stats(ostat[:, 2 * k + b, :], o[:, k, HS * b:HS * b + HS])
                    link(ins, S_["post0"], p0)
                    for b in range(2):
                        ins = v.bn_aggr(omv[:, 2 * k + b, :], ostat[:, 2 * k + b, :])
                    ins.then_inc(S_["ov"], 1)

            def half_normalise(u):
                p0 = post_count
                for k in range(2):
                    v.wait_ge(S_["os"], 2 * u + k + 1)
                    link(v.reciprocal(ors[:, 2 * k:2 * k + 2], osd[:, 2 * k:2 * k + 2]), S_["post0"], p0)
                    for b in range(2):
                        i = 2 * k + b
                        v.tensor_scalar(yn[:, u, i, :], o[:, k, HS * b:HS * b + HS], omv[:, i, 0:1], ors[:, i:i + 1],
                                        ALU.subtract, ALU.mult).then_inc(S_["yn"], 1)

            def gate_rows():
                for f in range(NF):
                    v.wait_ge(S_["o"], f + 1)
                    v.wait_ge(S_["g"], f + 1)
                    v.tensor_tensor(G[:, f, :], bank[f_bank(f)][:, 256:512], G[:, f, :], ALU.mult).then_inc(S_["res"], 1)

            post_count = [0]
            rates_to_pairs(0)
            v.wait_ge(S_["pair0"], 1)
            group_to_pairs(0, bank[6]).then_inc(S_["pair0T"], 1)
            v.wait_ge(S_["sig"], 1)
            v.wait_ge(S_["pool0"], 2)
            v.wait_ge(S_["pair0T"], 1)
            group(0, 0, lambda: upper_half(1))

            def routing():
                rates_to_pairs(1)
                route_gap()

            group(1, 1, routing, route_weights)
            v.wait_ge(S_["sig"], 2)
            with v.Fori(0, 4, 2) as i:
                group(i + 2, 0)
                group(i + 3, 1)
            group(6, 0)
            group(7, 1, last=True)
            half_variance(0)
            half_out_rows(0)
            half_variance(1)
            half_normalise(0)
            half_out_rows(1)
            half_normalise(1)
            gate_rows()

        @block.tensor
        def _(pe):
            pe.wait_ge(S_["warm"], 1)
            for _ in range(10):
                pe.matmul(bank[3][:, 0:256], pe_warm[:, 0:P], pe_warm[:, :], start=True, stop=True)
            pe.wait_ge(S_["small"], 16)

            def xn_channels(u):
                for k in range(KC):
                    for jj in range(4):
                        j = 4 * u + jj
                        pe.wait_ge(S_["xn"], j + 1)
                        ins = pe.transpose(bank[4 + 2 * u + k][:, P * jj:P * jj + P], xn[:, j, P * k:P * k + P], ident)
                    ins.then_inc(S_["xnT"], 1)

            def channels(w, base, u, name, first=0, end=4):
                for hf in range(KC):
                    for k in range(KC):
                        ins = pe.matmul(bank[base + hf][:, P * first:P * end], w[:, k, P * hf:P * hf + P],
                                        xnT[:, k, 4 * u + first:4 * u + end, :].rearrange("p j t -> p (j t)"),
                                        start=(k == 0), stop=(k == KC - 1))
                    ins.then_inc(S_[name], 1)

            def rates(u):
                for j in range(4 * u, 4 * u + 4):
                    for k in range(KC):
                        ins = pe.matmul(bank[7][:, NH * j:NH * j + NH], xnT[:, k, j, :], wlr[:, k, :],
                                        start=(k == 0), stop=(k == KC - 1))
                ins.then_inc(S_["eta"], 1)

            def pair_rows(j, bk):
                for hf in range(KC):
                    pe.transpose(bk[:, P * hf:P * hf + P], xkT[:, hf, j, :], ident)
                for k in range(KC):
                    pe.matmul(bk[:, 256:512], xnT[:, k, j, :], wt[:, k, :], start=(k == 0), stop=False)
                return pe.matmul(bk[:, 256:512], ones_row[:, :], grow[0:1, :], start=False, stop=True)

            def tile(j, i):
                c = 5 * j + i
                bk = bank[2 + c % 2]
                if i == 2 and j + 1 < NG:
                    pe.wait_ge(S_["pair_done"], j + 1)
                elif i == 2:
                    pass
                elif c >= 2:
                    pe.wait_ge(S_["scored"], 4 * j + i - 2 if i > 2 else 4 * (j - 1) + 3 + i)
                if i == 0:
                    pair_rows(j + 1, bk).then_inc(S_["pair"], 1)
                else:
                    q = i - 1
                    pe.wait_ge(S_["queries"], 4 * (j + 1))
                    for hf in range(KC):
                        for b in range(B):
                            ins = pe.matmul(bk[32 * b:32 * b + 32, P * hf:P * hf + P],
                                            xkT[32 * q:32 * q + 32, hf, j, GT * b:GT * b + GT],
                                            xqm[32 * q:32 * q + 32, j % 2, hf, b, :, :].rearrange("p h t -> p (h t)"),
                                            start=True, stop=True)
                    ins.then_inc(S_["sc"], 1)

            def query_rows(u):
                pe.wait_ge(S_["qchc"], 2 * (u + 1))
                if u:
                    pe.wait_ge(S_["rowsc"], 2)
                for hf in range(KC):
                    for b in range(B):
                        ins = pe.transpose(bank[4 + hf][:, P * b:P * b + P], xqT[:, hf, b, P * u:P * u + P], ident)
                    ins.then_inc(S_["rows"], 1)

            def expert_slot(i):
                if i < NS:
                    f, e = divmod(i, 4)
                    u, b = divmod(f, B)
                    if i >= 2:
                        pe.wait_ge(S_["gact"], 3 * (i - 1))
                    else:
                        pe.wait_ge(S_["rowsc"], 4)
                        pe.wait_ge(S_["split"], 3)
                        pe.wait_ge(S_["hi"], 3)
                    terms = [(x, w, k) for k in range(KC) for x, w in ((xnL_hi, gup_hi), (xnL_hi, gup_lo), (xnL_lo, gup_hi))]
                    for n, (x, w, k) in enumerate(terms):
                        ins = pe.matmul(bank[4 + i % 2][:, :], x[:, k, b, P * u:P * u + P].bitcast(F32R),
                                        w[:, k, 2 * e:2 * e + 2, :].rearrange("p e i -> p (e i)").bitcast(F32R),
                                        start=(n == 0), stop=(n == len(terms) - 1))
                    ins.then_inc(S_["gu"], 1)
                if 1 <= i <= NS:
                    pe.wait_ge(S_["h"], i)
                    if i >= 2:
                        pe.wait_ge(S_["hT"], i - 1)
                    for r in range(2):
                        ins = pe.transpose(bank[6][:, P * r:P * r + P], hh[:, (i - 1) % 2, r, :], ident)
                    ins.then_inc(S_["hTp"], 1)
                if i >= 2:
                    f, e = divmod(i - 2, 4)
                    pe.wait_ge(S_["hT"], i - 1)
                    if i == 2:
                        pe.wait_ge(S_["down"], 16)
                    if e == 0 and f:
                        pe.wait_ge(S_["g"], f)
                    for r in range(2):
                        ins = pe.matmul(bank[7][:, 0:HS], hT[:, i % 2, r, :], down[:, 2 * e + r, :],
                                        start=(e == 0 and r == 0), stop=(e == 3 and r == 1))
                    ins.then_inc(S_["y"], 1)

            def group_start(j):
                pe.wait_ge(S_["w_loaded"], 16 * (j + 1))
                if j == 0:
                    pe.wait_ge(S_["qchc"], 4)
                if j == 4:
                    pe.wait_ge(S_["zc"], 4)
                rows_j = slice(32 * (j % 4), 32 * (j % 4) + 32)
                for hf in range(KC):
                    for b in range(B):
                        ins = pe.matmul(bank[hf][rows_j, :].rearrange("p (h b d) -> p h b d", b=B, d=HD)[:, :, b, :],
                                        xqT[:, hf, b, GT * j:GT * j + GT], wblk[:, j % 2, KC * b + hf, :],
                                        start=(b == 0), stop=False, skip_group_check=True)
                ins.then_inc(S_["z0"], 1)

            def group_end(j):
                pe.wait_ge(S_["masked"], 4 * (j + 1))
                rows_j = slice(32 * (j % 4), 32 * (j % 4) + 32)
                for h in range(NH):
                    hf, r = divmod(h, HH)
                    q, c = r // 4, GT * (4 * hf + r % 4)
                    if r == 0:
                        pe.wait_ge(S_["sgp"], 2 * j + hf + 1)
                    ins = pe.matmul(bank[hf][rows_j, 4 * HD * r:4 * HD * r + 4 * HD], A[:, j % 2, q, c:c + GT],
                                    sgpad[:, j % 2, h, :, :].rearrange("p b d -> p (b d)"),
                                    start=False, stop=(j % 4 == 3 and r == HH - 1), skip_group_check=True)
                    if r == HH - 1:
                        ins.then_inc(S_["z"], 1)

            def half_bias(u):
                pe.wait_ge(S_["b_saved"], 256 * (u + 1))
                for k in range(2):
                    pe.matmul(bank[k][:, :], sel, biasr[:, u, 512 * k:512 * k + 512],
                              start=False, stop=False, skip_group_check=True)

            def post_channels(f):
                pe.wait_ge(S_["yn"], f + 1)
                if f >= 4:
                    pe.wait_ge(S_["res"], f - 3)
                for k in range(KC):
                    ins = pe.transpose(bank[f_bank(f)][:, P * k:P * k + P], yn[:, f // 4, f % 4, P * k:P * k + P], ident)
                ins.then_inc(S_["yTp"], 1)

            def project(f):
                pe.wait_ge(S_["yT"], 2 * (f + 1))
                for k in range(KC):
                    ins = pe.matmul(bank[f_bank(f)][:, 256:512], yT[:, f % 2, k, :], wo[:, k, :],
                                    start=(k == 0), stop=(k == KC - 1))
                ins.then_inc(S_["o"], 1)

            xn_channels(0)
            pe.wait_ge(S_["wkv"], 16)
            pe.wait_ge(S_["xnTc"], 2)
            channels(wk, 2, 0, "kch", 0, 1)
            pe.wait_ge(S_["wlr"], 16)
            rates(0)
            pe.wait_ge(S_["kchc"], 2)
            pe.wait_ge(S_["wt"], 1)
            pair_rows(0, bank[6]).then_inc(S_["pair0"], 1)
            channels(wk, 0, 0, "kch", 1, 4)
            pe.wait_ge(S_["wq"], 16)
            pe.wait_ge(S_["kchc"], 4)
            tile(0, 0)
            channels(wq, 0, 0, "qch")
            pe.wait_ge(S_["pair0T"], 1)
            xn_channels(1)
            pe.wait_ge(S_["qchc"], 2)
            pe.wait_ge(S_["xnTc"], 4)
            channels(wk, 0, 1, "kch")
            tile(0, 1)
            tile(0, 2)
            rates(1)
            tile(0, 3)
            query_rows(0)
            tile(0, 4)
            tile(1, 0)
            pe.wait_ge(S_["kchc"], 6)
            channels(wq, 0, 1, "qch")
            pe.wait_ge(S_["wrt"], 16)
            pe.wait_ge(S_["xnTc"], 8)
            for f in range(NF):
                u, b = divmod(f, B)
                for k in range(KC):
                    ins = pe.matmul(bank[6][:, 256 + f * NE:256 + (f + 1) * NE], xnL[:, k, b, P * u:P * u + P],
                                    wrt[:, k, :], start=(k == 0), stop=(k == KC - 1))
            ins.then_inc(S_["route"], 1)
            query_rows(1)
            slot = 0
            for j in range(1, NG):
                last = slot + SLOTS[j]
                tile(j, 1)
                expert_slot(slot)
                tile(j, 2)
                if j != 5:
                    group_start(j - 1)
                tile(j, 3)
                expert_slot(slot + 1)
                tile(j, 4)
                if j + 2 < NG:
                    tile(j + 1, 0)
                for i in range(slot + 2, last):
                    expert_slot(i)
                if j == 5:
                    group_start(4)
                if j == 4:
                    half_bias(0)
                group_end(j - 1)
                slot = last
            group_start(NG - 1)
            half_bias(1)
            pe.wait_ge(S_["wo"], 16)
            for i in range(slot, NS):
                expert_slot(i)
                if i == slot:
                    group_end(NG - 1)
            pe.wait_ge(S_["gact"], 3 * NS)
            for f in range(4):
                post_channels(f)
            expert_slot(NS)
            expert_slot(NS + 1)
            for f in range(4):
                project(f)
            for f in range(4, NF):
                post_channels(f)
            for f in range(4, NF):
                project(f)


def kernel(**inputs):
    import numpy as np
    import concourse.bacc as bacc
    from concourse.bass_utils import run_bass_kernel_spmd

    a = {k: np.ascontiguousarray(w) for k, w in inputs.items()}

    def in_major(w):
        return w.T.reshape(KC, P, -1).transpose(1, 0, 2)

    def rep(w):
        return np.broadcast_to(w.reshape(1, -1), (P, w.size))

    def pairs(w):
        return np.broadcast_to(w.reshape(1, NH, -1), (B, NH, w.size // NH)).reshape(P, -1)

    def half_tiles(x):
        return x.reshape(B, 2, P, HS).transpose(2, 1, 0, 3).reshape(P, NF, HS)

    x = a["L0_attn_hidden_states"]
    gu = a["L0_ffn_expert_gate_up"].reshape(NE, KC, P, NI, 2).transpose(2, 1, 0, 4, 3).reshape(P, KC, NE, 2 * NI)
    p = np.arange(P)
    s, t = p[:, None] % GT, np.arange(GT)[None, :]
    parts = {
        "gam": pairs(a["L0_attn_ttt_norm_weight"]), "bet": pairs(a["L0_attn_ttt_norm_bias"]),
        "w0": np.concatenate([pairs(a["L0_attn_W1"]), pairs(a["L0_attn_b1"])], 1),
        "lrb": pairs(a["L0_attn_ttt_lr_bias"]),
        "gam_row": rep(a["L0_attn_ttt_norm_weight"]), "bet_row": rep(a["L0_attn_ttt_norm_bias"]),
        "lti": rep(a["L0_attn_learnable_token_idx"]), "inv": rep(1.0 / np.arange(1, K + 1)),
        "iota": rep(np.arange(NE)), "bmask": p[:, None] // GT == np.arange(4)[None, :],
        "cmask": p[:, None] // HD % 4 == np.arange(4)[None, :],
        "mask_tok": ((s // K == t // K) & (s <= t)) * (-1.0 / HD), "mask_last": (s // K < t // K) * (-1.0 / HD),
        "post_w": a["L0_attn_post_norm_weight"].reshape(KC, P).T,
        "post_b": a["L0_attn_post_norm_bias"].reshape(KC, P).T,
        "ident": np.eye(P), "sel": p[:, None] == p[None, :] // GT,
    }
    arrays = {
        "x_bt": x.reshape(B, NG, GT, HS).transpose(0, 2, 1, 3).reshape(P, NG, HS), "x_tok": half_tiles(x),
        "small": np.concatenate([np.asarray(parts[k], np.float32) for k in SMALL], 1),
        "wkv": np.stack([in_major(a["L0_attn_k_w"]), in_major(a["L0_attn_v_w"])], 1),
        "wq": in_major(a["L0_attn_q_w"]),
        "wlr": in_major(a["L0_attn_ttt_lr_weight"].reshape(NH, HS)), "wrt": in_major(a["L0_ffn_router_gate"]),
        "gup": gu.reshape(P, KC, NE * 2 * NI), "down": a["L0_ffn_expert_down"].transpose(1, 0, 2), "wo": in_major(a["L0_attn_o_w"]),
    }
    arrays = {f"in_{k}": np.ascontiguousarray(w, dtype=np.float32) for k, w in arrays.items()}
    nc = bacc.Bacc("TRN2", target_bir_lowering=False, num_devices=1)
    aps = [nc.dram_tensor(k, w.shape, F32, kind="ExternalInput").ap() for k, w in arrays.items()]
    out = nc.dram_tensor("out", (P, NF, HS), F32, kind="ExternalOutput").ap()
    build(nc, *aps, out)
    r = run_bass_kernel_spmd(nc, [arrays], core_ids=[0])
    return r.results[0]["out"].reshape(P, 2, B, HS).transpose(2, 1, 0, 3).reshape(B, L, HS)
```
